# Optimizing a Trainium2 kernel written in Bass

```python
import numpy as np
import jax
import jax.numpy as jnp

def _softmax(x, axis=-1):
    return jax.nn.softmax(x, axis=axis)

def _gelu(x):
    return jax.nn.gelu(x, approximate=True)

def _silu(x):
    return jax.nn.silu(x)

def _sigmoid(x):
    return jax.nn.sigmoid(x)

def _layernorm(x, axis=-1, eps=1e-05):
    m = jnp.mean(x, axis=axis, keepdims=True)
    v = jnp.var(x, axis=axis, keepdims=True)
    return (x - m) / jnp.sqrt(v + eps)

def _scatter_add(tgt, idx, src, axis=0):
    return tgt.at[idx].add(src)

def _segment_sum(src, seg, n):
    return jax.ops.segment_sum(src, seg, n)
kernel_name = 'mk_gnn_preln_d2_gnn_r8_50a306'

def setup_inputs(seed: int=0):
    np.random.seed(seed)
    _w = jnp.asarray

    def _rec_inputs():
        import jax
        import jax.numpy as jnp
        _gk = jax.random.key(seed)
        x = 7.22e-05 + 1 * jax.random.normal(jax.random.fold_in(_gk, 1), (6250, 128), jnp.float32)
        _s = jax.random.randint(jax.random.fold_in(_gk, 2), (50000,), 0, 6250, jnp.int32)
        _d = jax.random.randint(jax.random.fold_in(_gk, 3), (50000,), 0, 6250, jnp.int32)
        _loop = jnp.arange(6250, dtype=jnp.int32)
        src = jnp.concatenate([_s, _d, _loop])
        dst = jnp.concatenate([_d, _s, _loop])
        _o = jnp.argsort(dst, stable=True)
        src = src[_o]
        dst = dst[_o]
        edge_attr_128 = 2.93046e-05 + 1.00006 * jax.random.normal(jax.random.fold_in(_gk, 11), (106250, 128), jnp.float32)
        return (x, src, dst, edge_attr_128)
    x, src, dst, edge_attr_128 = _rec_inputs()

    def _L0_gnn_setup():
        import jax, jax.numpy as jnp
        import numpy as np
        N_NODES = 8192
        N_EDGES = 65536
        D = 128
        N_LAYERS = 3
        LN_EPS = 1e-05

        def _layernorm(h, g, b):
            mu = jnp.mean(h, axis=-1, keepdims=True)
            var = jnp.mean(jnp.square(h - mu), axis=-1, keepdims=True)
            return (h - mu) * jax.lax.rsqrt(var + LN_EPS) * g + b
        key = jax.random.key(seed)
        ks = jax.random.split(key, 10)
        x = jax.random.normal(ks[0], (N_NODES, D), dtype=jnp.float32)
        edge_index = jax.random.randint(ks[1], (2, N_EDGES), 0, N_NODES, dtype=jnp.int64)
        s = 1.0 / np.sqrt(D)
        lin_w = jax.random.normal(ks[2], (N_LAYERS, D, D), dtype=jnp.float32) * s
        lin_b = jax.random.normal(ks[3], (N_LAYERS, D), dtype=jnp.float32) * s
        linl_w = jax.random.normal(ks[4], (N_LAYERS, D, D), dtype=jnp.float32) * s
        linl_b = jax.random.normal(ks[5], (N_LAYERS, D), dtype=jnp.float32) * s
        linr_w = jax.random.normal(ks[6], (N_LAYERS, D, D), dtype=jnp.float32) * s
        ln_g = jnp.ones((N_LAYERS - 1, D), dtype=jnp.float32)
        ln_b = jnp.zeros((N_LAYERS - 1, D), dtype=jnp.float32)
        return {'x': x, 'edge_index': edge_index, 'lin_w': lin_w, 'lin_b': lin_b, 'linl_w': linl_w, 'linl_b': linl_b, 'linr_w': linr_w, 'ln_g': ln_g, 'ln_b': ln_b}
    _L0_gnn_all = _L0_gnn_setup()
    _L0_gnn_in = {k: v for k, v in _L0_gnn_all.items() if k in ('lin_w', 'lin_b', 'linl_w', 'linl_b', 'linr_w', 'ln_g', 'ln_b')}
    del _L0_gnn_all

    def _L1_gnn_setup():
        import jax, jax.numpy as jnp
        import numpy as np
        N = 6250
        E = 80000
        D = 128

        def _lin_init(key, fan_in, fan_out):
            kw, kb = jax.random.split(key)
            bound = 1.0 / np.sqrt(fan_in)
            W = jax.random.uniform(kw, (fan_in, fan_out), jnp.float32, -bound, bound)
            b = jax.random.uniform(kb, (fan_out,), jnp.float32, -bound, bound)
            return (W, b)
        key = jax.random.key(seed)
        ks = jax.random.split(key, 7)
        x = jax.random.normal(ks[0], (N, D), jnp.float32)
        edge_index = jax.random.randint(ks[1], (2, E), 0, N, dtype=jnp.int64)
        edge_attr = jax.random.normal(ks[2], (E, D), jnp.float32)
        msg_w1, msg_b1 = _lin_init(ks[3], 3 * D, D)
        msg_w2, msg_b2 = _lin_init(ks[4], D, D)
        upd_w1, upd_b1 = _lin_init(ks[5], 2 * D, D)
        upd_w2, upd_b2 = _lin_init(ks[6], D, D)
        return {'x': x, 'edge_index': edge_index, 'edge_attr': edge_attr, 'msg_w1': msg_w1, 'msg_b1': msg_b1, 'msg_w2': msg_w2, 'msg_b2': msg_b2, 'upd_w1': upd_w1, 'upd_b1': upd_b1, 'upd_w2': upd_w2, 'upd_b2': upd_b2}
    _L1_gnn_all = _L1_gnn_setup()
    _L1_gnn_in = {k: v for k, v in _L1_gnn_all.items() if k in ('msg_w1', 'msg_b1', 'msg_w2', 'msg_b2', 'upd_w1', 'upd_b1', 'upd_w2', 'upd_b2')}
    del _L1_gnn_all
    return {'x': x, 'src': src, 'dst': dst, 'edge_attr_128': edge_attr_128, 'L0_gnn_lin_w': _L0_gnn_in['lin_w'], 'L0_gnn_lin_b': _L0_gnn_in['lin_b'], 'L0_gnn_linl_w': _L0_gnn_in['linl_w'], 'L0_gnn_linl_b': _L0_gnn_in['linl_b'], 'L0_gnn_linr_w': _L0_gnn_in['linr_w'], 'L0_gnn_ln_g': _L0_gnn_in['ln_g'], 'L0_gnn_ln_b': _L0_gnn_in['ln_b'], 'L1_gnn_msg_w1': _L1_gnn_in['msg_w1'], 'L1_gnn_msg_b1': _L1_gnn_in['msg_b1'], 'L1_gnn_msg_w2': _L1_gnn_in['msg_w2'], 'L1_gnn_msg_b2': _L1_gnn_in['msg_b2'], 'L1_gnn_upd_w1': _L1_gnn_in['upd_w1'], 'L1_gnn_upd_b1': _L1_gnn_in['upd_b1'], 'L1_gnn_upd_w2': _L1_gnn_in['upd_w2'], 'L1_gnn_upd_b2': _L1_gnn_in['upd_b2']}

def reference(x, src, dst, edge_attr_128, L0_gnn_lin_w, L0_gnn_lin_b, L0_gnn_linl_w, L0_gnn_linl_b, L0_gnn_linr_w, L0_gnn_ln_g, L0_gnn_ln_b, L1_gnn_msg_w1, L1_gnn_msg_b1, L1_gnn_msg_w2, L1_gnn_msg_b2, L1_gnn_upd_w1, L1_gnn_upd_b1, L1_gnn_upd_w2, L1_gnn_upd_b2):
    import jax
    import jax.numpy as jnp

    def _L0_gnn_ref(x, edge_index, lin_w, lin_b, linl_w, linl_b, linr_w, ln_g, ln_b):
        import jax, jax.numpy as jnp
        import numpy as np
        N_NODES = 8192
        N_EDGES = 65536
        D = 128
        N_LAYERS = 3
        LN_EPS = 1e-05

        def _layernorm(h, g, b):
            mu = jnp.mean(h, axis=-1, keepdims=True)
            var = jnp.mean(jnp.square(h - mu), axis=-1, keepdims=True)
            return (h - mu) * jax.lax.rsqrt(var + LN_EPS) * g + b
        n = x.shape[0]
        src, dst = (edge_index[0], edge_index[1])
        cnt = jax.ops.segment_sum(jnp.ones_like(dst, dtype=x.dtype), dst, num_segments=n)
        cnt = jnp.maximum(cnt, 1.0)[:, None]
        for i in range(N_LAYERS):
            xp = jax.nn.relu(x @ lin_w[i].T + lin_b[i])
            msg = xp[src]
            agg = jax.ops.segment_sum(msg, dst, num_segments=n) / cnt
            h = agg @ linl_w[i].T + linl_b[i] + x @ linr_w[i].T
            if i != N_LAYERS - 1:
                h = _layernorm(jax.nn.relu(h), ln_g[i], ln_b[i])
            x = h
        return x

    def _L1_gnn_ref(x, edge_index, edge_attr, msg_w1, msg_b1, msg_w2, msg_b2, upd_w1, upd_b1, upd_w2, upd_b2):
        import jax, jax.numpy as jnp
        import numpy as np
        N = 6250
        E = 80000
        D = 128

        def _lin_init(key, fan_in, fan_out):
            kw, kb = jax.random.split(key)
            bound = 1.0 / np.sqrt(fan_in)
            W = jax.random.uniform(kw, (fan_in, fan_out), jnp.float32, -bound, bound)
            b = jax.random.uniform(kb, (fan_out,), jnp.float32, -bound, bound)
            return (W, b)
        row, col = (edge_index[0], edge_index[1])
        num_nodes = x.shape[0]
        m_in = jnp.concatenate([x[row], x[col], edge_attr], axis=-1)
        h = jax.nn.relu(m_in @ msg_w1 + msg_b1)
        messages = h @ msg_w2 + msg_b2
        summed = jax.ops.segment_sum(messages, col, num_segments=num_nodes)
        counts = jax.ops.segment_sum(jnp.ones((messages.shape[0],), messages.dtype), col, num_segments=num_nodes)
        aggregated = jnp.where(counts[:, None] > 0, summed / jnp.maximum(counts, 1.0)[:, None], jnp.zeros_like(summed))
        u_in = jnp.concatenate([x, aggregated], axis=-1)
        updated = jax.nn.relu(u_in @ upd_w1 + upd_b1) @ upd_w2 + upd_b2
        return updated
    edge_index = jnp.stack([src, dst])
    h = jnp.maximum(_layernorm(x, axis=-1), 0.0)
    x = x + _L0_gnn_ref(h, edge_index, L0_gnn_lin_w, L0_gnn_lin_b, L0_gnn_linl_w, L0_gnn_linl_b, L0_gnn_linr_w, L0_gnn_ln_g, L0_gnn_ln_b)
    h = jnp.maximum(_layernorm(x, axis=-1), 0.0)
    x = x + _L1_gnn_ref(h, edge_index, edge_attr_128, L1_gnn_msg_w1, L1_gnn_msg_b1, L1_gnn_msg_w2, L1_gnn_msg_b2, L1_gnn_upd_w1, L1_gnn_upd_b1, L1_gnn_upd_w2, L1_gnn_upd_b2)
    return x

_drawn_inputs = setup_inputs


def setup_inputs(seed=0):
    import zlib

    import numpy as np

    out = dict(_drawn_inputs(seed))
    spreads = {'L0_gnn_ln_g': (1.0, 0.2), 'L0_gnn_ln_b': (0.0, 0.1)}
    factors = {'edge_attr_128': 8.0,
     'L1_gnn_msg_w1': 5.943,
     'L1_gnn_msg_b1': 34.278,
     'L1_gnn_msg_w2': 3.888,
     'L1_gnn_msg_b2': 24.441,
     'L1_gnn_upd_b1': 5.845,
     'L1_gnn_upd_b2': 3.952}
    for name, (base, spread) in spreads.items():
        noise = np.random.default_rng([zlib.crc32(name.encode()), seed]).standard_normal(out[name].shape)
        drawn = base * np.exp(spread * noise) if base else spread * noise
        out[name] = jnp.asarray(drawn.astype(out[name].dtype))
    for name, factor in factors.items():
        out[name] = (out[name] * factor).astype(out[name].dtype)
    return out
```

```python
from contextlib import ExitStack

import numpy as np

import concourse.bass as bass
from concourse import mybir

N, D, E = 6250, 128, 106250
P = 128
NT = -(-N // P)
NPAD = NT * P
K = 8
GE = P * K
RING = 4
NG = RING * (-(-E // (GE * RING)))
EPAD = NG * GE
SUPER = NG // RING
TB = 7
NB = NT // TB
BW = TB * P
assert NB * TB == NT
EPS = 1e-5

F32, BF16, I32 = mybir.dt.float32, mybir.dt.bfloat16, mybir.dt.int32
ALU, ACT, AX = mybir.AluOpType, mybir.ActivationFunctionType, mybir.AxisListType

C_IOTA, C_BASE, C_NODE, C_ID, C_END = 0, P, P + NT, P + 2 * NT, 2 * P + 2 * NT

MATS = ["lin0", "lin1", "lin2", "wl0", "wl1", "wl2", "wr0", "wr1", "wr2",
        "m_src", "m_dst", "m_edge", "m_w2", "u_x", "u_agg", "u_w2"]
ROWS = ["lin_b0", "lin_b1", "lin_b2", "wl_b0", "wl_b1", "wl_b2", "m_b1", "m_b2", "u_b2"]
COLS = ["g0", "g1", "b0", "b1", "u_b1"]

STEPS = {
    "mean": (1, 2, 3, 4), "proj": (1, 2, 3, 4), "sum": (1, 2, 3), "relu": (1, 2), "stats": (0, 1, 2, 3),
    "std": (0, 1, 2, 3), "rstd": (0, 1, 2, 3), "norm": (0, 1, 2, 3), "turn": (0, 1, 2, 3), "feat": (0, 1, 2, 3),
    "table": (0, 1, 2, 3), "own": (0, 1, 2, 3), "tabout": (0, 1, 2, 3), "ownout": (0, 1, 2, 3),
    "upx": (3,), "upxout": (3,), "aggd": (4,), "uagg": (4,), "usum": (4,), "urelu": (4,), "out": (4,),
    "outsb": (4,),
}


def done(step, phase, b):
    return NB * sum(q < phase for q in STEPS[step]) + b + 1


def gnn_kernel(nc, x, src, dst, dst_t, dst_g, edge_attr, consts, mats, rows, cols, out):
    ctx = ExitStack()
    with ctx:
        def sb(name, shape, dt=F32):
            return ctx.enter_context(nc.sbuf_tensor(name, shape, dt))

        def sem(name):
            return ctx.enter_context(nc.semaphore(name))

        table = nc.dram_tensor("table", (NPAD, D), F32).ap()
        x1_dram = nc.dram_tensor("x1_dram", (NPAD, D), F32).ap()
        win_dram = nc.dram_tensor("win_dram", (NG, 2), I32).ap()

        con = sb("con", [P, C_END])
        mat = sb("mat", [P, len(MATS), D])
        row = sb("row", [1, len(ROWS), D])
        col = sb("col", [P, len(COLS)])
        ones_row = sb("ones_row", [1, P])
        ones = sb("ones", [P, P])
        zeros = sb("zeros", [P, P])
        eps = sb("eps", [P, 1])
        dst_i = sb("dst_i", [P, NG * K], I32)
        dst_f = sb("dst_f", [P, NG * K])
        win_m = sb("win_m", [NG, 2], I32)
        win_s = sb("win_s", [NG, 2], I32)
        win = sb("win", [1, 2 * NG], I32)

        agg = sb("agg", [P, NPAD])
        cnt = sb("cnt", [P, NPAD])
        own = sb("own", [P, NPAD])
        q_parts = sb("q_parts", [P, 3, NPAD], BF16)

        idx = sb("idx", [P, RING, K], I32)
        rows_g = sb("rows_g", [P, RING, K, D])
        onehot = sb("onehot", [P, 2, K, P])
        buf = sb("buf", [P, 8 * GE])
        dst_g_sb = buf[0:NG, 0:GE].bitcast(I32)
        mean, z, zr, y, feat, stage, extra = (buf[:, i * GE:i * GE + BW] for i in range(7))
        ind = buf[0:1, 7 * GE:7 * GE + BW]
        ea = [buf[:, i * GE:(i + 1) * GE] for i in range(2)]
        eat = buf[:, 2 * GE:3 * GE]
        dtb = [buf[:, i * GE:(i + 1) * GE].bitcast(I32) for i in (3, 4)]
        msg = [buf[:, i * GE:(i + 1) * GE] for i in (5, 6)]
        onehot_t = buf[:, 7 * GE:8 * GE].bitcast(BF16).rearrange("p (s e) -> p s e", s=2)
        st6 = sb("st6", [P, TB, 6])
        mv = sb("mv", [P, TB, 2])
        std = sb("std", [P, TB])
        rstd = sb("rstd", [P, TB])

        def pb(name):
            return ctx.enter_context(nc.psum_tensor(name, [P, GE], F32))

        ps_h, ps_t, ps_x, ps_b = pb("ps_h"), pb("ps_t"), pb("ps_x"), pb("ps_b")
        ps_m = [ps_x, ps_b]
        ps_a = ps_h[:, :].rearrange("p (s c) -> p s c", s=2)
        ps_c = ps_t[:, :].rearrange("p (s c) -> p s c", s=2)

        in_const = sem("in_const")
        in_dst = sem("in_dst")
        in_dstg = sem("in_dstg")
        ready = sem("ready")
        win_made = sem("win_made")
        win_out = sem("win_out")
        win_in = sem("win_in")
        st = {k: sem("n_" + k) for k in STEPS}
        chain = sem("chain")
        x_in = sem("x_in")
        tab_out = sem("tab_out")
        x1_out = sem("x1_out")
        ind_made = sem("ind_made")
        final_out = sem("final_out")
        idx_in = [sem(f"idx_in{s}") for s in range(RING)]
        gathered = [sem(f"gathered{s}") for s in range(RING)]
        passed = sem("passed")
        rows_used = sem("rows_used")
        hot = sem("hot")
        aggd = sem("aggd")
        added = sem("added")
        pass_done = sem("pass_done")
        ea_in = [sem("ea_in0"), sem("ea_in1")]
        dt_in = [sem("dt_in0"), sem("dt_in1")]
        turned = sem("turned")
        eat_made = sem("eat_made")
        hot_t = sem("hot_t")
        q_added = sem("q_added")
        m_done = sem("m_done")
        m_sum = sem("m_sum")
        m_relu = sem("m_relu")
        msg_used = sem("msg_used")

        M = {k: mat[:, i, :] for i, k in enumerate(MATS)}
        R = {k: row[0:1, i, :] for i, k in enumerate(ROWS)}
        C = {k: col[:, i:i + 1] for i, k in enumerate(COLS)}
        ident = con[:, C_ID:C_ID + P]

        def blk(t, b):
            return t[:, bass.ds(b * BW, BW)]

        def dram_blk(t, b):
            return t[bass.ds(b * BW, BW), :].rearrange("(t p) f -> p t f", p=P)

        def tiles(t):
            return t.rearrange("p (t f) -> p t f", f=P)

        def windows(eng, g):
            lo = eng.value_load(win[0:1, bass.ds(2 * g, 1)], min_val=0, max_val=NT - 1)
            hi = eng.value_load(win[0:1, bass.ds(2 * g + 1, 1)], min_val=1, max_val=NT)
            return lo, hi

        block = ctx.enter_context(nc.Block())

        @block.sync
        def _(sp):
            sp.dma_start(con[:, :], consts).then_inc(in_const, 16)
            sp.dma_start(mat[:, :, :], mats).then_inc(in_const, 16)
            sp.dma_start(row[:, :, :], rows).then_inc(in_const, 16)
            sp.dma_start(col[:, :], cols).then_inc(in_const, 16)
            sp.dma_start(dst_g_sb, dst_g).then_inc(in_dstg, 16)
            sp.dma_start(dst_i[:, :], dst).then_inc(in_dst, 16)
            sp.wait_ge(win_made, 1)
            sp.dma_start(win_dram, win_s[:, :]).then_inc(win_out, 16)
            sp.wait_ge(win_out, 16)
            sp.dma_start(win[:, :], win_dram.rearrange("(o g) c -> o (g c)", o=1)).then_inc(win_in, 16)

            def store_table(phase, b):
                sp.wait_ge(st["tabout"], done("tabout", phase, b))
                sp.sem_inc(passed, 1)
                sp.dma_start(dram_blk(table, b), tiles(stage)).then_inc(tab_out, 16)

            sp.dma_start(tiles(z), dram_blk(x, 0)).then_inc(x_in, 16)
            with sp.Fori(1, NB) as b:
                sp.wait_ge(st["norm"], done("norm", 0, b - 1))
                sp.sem_inc(passed, 1)
                sp.dma_start(tiles(z), dram_blk(x, b)).then_inc(x_in, 16)
                store_table(0, b - 1)
            store_table(0, NB - 1)

            for l in range(4):
                if l == 3:
                    sp.wait_ge(st["upx"], done("upx", 3, NB - 1))
                    sp.wait_ge(st["table"], done("table", 3, NB - 1))
                    sp.wait_ge(st["own"], done("own", 3, NB - 1))
                    sp.wait_ge(st["ownout"], done("ownout", 3, NB - 1))
                    sp.wait_ge(st["tabout"], done("tabout", 3, NB - 1))
                    sp.wait_ge(x1_out, 16 * NB)
                with sp.Fori(0, SUPER) as j:
                    for s in range(RING):
                        g = j * RING + s
                        sp.wait_ge(gathered[s], (l * SUPER + j) * 16 * K)
                        sp.sem_inc(passed, 1)
                        sp.dma_start(idx[:, s, :], src[:, bass.ds(g * K, K)]).then_inc(idx_in[s], 16)
                        if l == 3:
                            sp.wait_ge(turned, g + 1)
                            sp.sem_inc(passed, 1)
                            sp.dma_start(ea[s % 2].rearrange("p (k f) -> p k f", f=D),
                                         edge_attr[bass.ds(g * GE, GE), :].rearrange("(p k) f -> p k f", k=K)) \
                                .then_inc(ea_in[s % 2], 16)
                            sp.wait_ge(m_done, g + 1)
                            sp.sem_inc(passed, 1)
                            sp.dma_start(dtb[s % 2], dst_t[bass.ds(g, 1), :].partition_broadcast(P)) \
                                .then_inc(dt_in[s % 2], 16)
                ph = l + 1
                if ph < 3:
                    with sp.Fori(0, NB) as b:
                        store_table(ph, b)
                elif ph == 3:
                    def load_x(b):
                        sp.wait_ge(st["sum"], done("sum", 3, b) - 1)
                        sp.sem_inc(passed, 1)
                        sp.dma_start(tiles(extra), dram_blk(x, b)).then_inc(x_in, 16)

                    load_x(0)
                    with sp.Fori(0, NB - 1) as b:
                        sp.wait_ge(st["sum"], done("sum", 3, b))
                        sp.sem_inc(passed, 1)
                        sp.dma_start(dram_blk(x1_dram, b), tiles(z)).then_inc(x1_out, 16)
                        load_x(b + 1)
                        store_table(3, b)
                    sp.wait_ge(st["sum"], done("sum", 3, NB - 1))
                    sp.sem_inc(passed, 1)
                    sp.dma_start(dram_blk(x1_dram, NB - 1), tiles(z)).then_inc(x1_out, 16)
                    store_table(3, NB - 1)
                else:
                    def load_x1(b):
                        sp.dma_start(tiles(extra), dram_blk(x1_dram, b)).then_inc(x_in, 16)

                    sp.wait_ge(pass_done, 4)
                    load_x1(0)
                    with sp.Fori(0, NB - 1) as b:
                        sp.wait_ge(st["outsb"], b + 1)
                        load_x1(b + 1)
                        sp.dma_start(dram_blk(out, b), tiles(stage)).then_inc(final_out, 16)
                    sp.wait_ge(st["outsb"], NB)
                    sp.dma_start(dram_blk(out, NB - 1), tiles(stage)).then_inc(final_out, 16)
            sp.wait_ge(final_out, 16 * NB)

        @block.gpsimd
        def _(pool):
            pool.sem_inc(rows_used, RING)
            pool.sem_inc(m_relu, RING)
            for l in range(4):
                pool.wait_ge(tab_out, 16 * NB * (l + 1))
                if l == 3:
                    pool.wait_ge(rows_used, 3 * NG + RING)
                with pool.Fori(0, SUPER) as j:
                    for s in range(RING):
                        if l < 3:
                            pool.wait_ge(rows_used, (l * SUPER + j) * RING + s + 1)
                        else:
                            pool.wait_ge(m_relu, j * RING + s + 1)
                        pool.wait_ge(idx_in[s], (l * SUPER + j + 1) * 16)
                        pool.sem_inc(passed, 1)
                        for k in range(K):
                            pool.indirect_dma_start(
                                rows_g[:, s, k, :], None, table,
                                bass.IndirectOffsetOnAxis(ap=idx[:, s, k:k + 1], axis=0),
                            ).then_inc(gathered[s], 16)

        @block.tensor
        def _(pe):
            visit = pe.alloc_register("pe_visit")
            qvisit = pe.alloc_register("pe_qvisit")
            pe.reg_mov(visit, 0)
            pe.reg_mov(qvisit, 0)
            pe.sem_inc(aggd, 2)
            pe.sem_inc(turned, 2)
            pe.sem_inc(q_added, 2)
            pe.sem_inc(m_done, 2)
            pe.sem_inc(msg_used, 2)
            pe.wait_ge(in_const, 64)
            pe.wait_ge(win_in, 16)
            pe.wait_ge(ready, 1)

            def signal(s, at, start=True):
                nc.tensor.matmul(at, zeros[0:1, 0:1], zeros[0:1, 0:1], start=start, stop=True,
                                 skip_group_check=not start).then_inc(s, 1)

            def zero_visit(l):
                v = pe.snap(visit, min_val=0, max_val=1 << 20)
                pe.wait_ge(added, v + 1)
                if l == 0:
                    nc.tensor.matmul(ps_c[:, bass.ds(v % 2, 1), 0:P], zeros[:, :], zeros[:, :], start=True, stop=True)
                nc.tensor.matmul(ps_a[:, bass.ds(v % 2, 1), 0:P], zeros[:, :], zeros[:, :],
                                 start=True, stop=True).then_inc(aggd, 1)
                pe.reg_add(visit, visit, 1)

            def agg_visits(l, g, rows_of, rows_sem, rows_value):
                lo, hi = windows(pe, g)
                pe.wait_ge(rows_sem, rows_value)
                pe.sem_inc(passed, 1)
                with pe.Fori(lo, hi):
                    v = pe.snap(visit, min_val=0, max_val=1 << 20)
                    pe.wait_ge(hot, v + 1)
                    pe.wait_ge(added, v + 1)
                    hs = onehot[:, bass.ds(v % 2, 1), :, :]
                    if l == 0:
                        for k in range(K):
                            nc.tensor.matmul(ps_c[:, bass.ds(v % 2, 1), 0:P], ones[:, :], hs[:, :, k, :],
                                             start=(k == 0), stop=(k == K - 1))
                    for k in range(K):
                        last = nc.tensor.matmul(ps_a[:, bass.ds(v % 2, 1), 0:P], rows_of(k), hs[:, :, k, :],
                                                start=(k == 0), stop=(k == K - 1))
                    last.then_inc(aggd, 1)
                    pe.reg_add(visit, visit, 1)

            def block_products(dst_ps, lhs, rhs, bias, s):
                for t in range(TB):
                    o = dst_ps[:, t * P:(t + 1) * P]
                    last = nc.tensor.matmul(o, lhs[:, t * P:(t + 1) * P], M[rhs], start=True, stop=bias is None)
                    if bias is not None:
                        last = nc.tensor.matmul(o, ones_row[0:1, :], R[bias], start=False, stop=True)
                last.then_inc(st[s], 1)

            HALF = [(0, 512), (512, BW)]

            for ph in range(4):
                with pe.Fori(0, NB) as b:
                    if ph:
                        pe.wait_ge(st["mean"], done("mean", ph, b))
                        pe.wait_ge(st["sum"], done("sum", ph, b) - 1)
                        if ph == 3:
                            pe.wait_ge(st["upxout"], b)
                        block_products(ps_h, mean, f"wl{ph - 1}", None, "proj")
                    pe.wait_ge(st["norm"], done("norm", ph, b))
                    pe.wait_ge(st["feat"], done("feat", ph, b) - 1)
                    for t in range(TB):
                        last = nc.tensor.transpose(ps_t[:, t * P:(t + 1) * P], y[:, t * P:(t + 1) * P], ident)
                    last.then_inc(st["turn"], 1)
                    pe.wait_ge(st["feat"], done("feat", ph, b))
                    pe.wait_ge(st["tabout"], done("tabout", ph, b) - 1)
                    tab_w, tab_b, own_w, own_b = (
                        (f"lin{ph}", f"lin_b{ph}", f"wr{ph}", f"wl_b{ph}") if ph < 3 else ("m_src", None, "m_dst", "m_b1"))
                    block_products(ps_x, feat, tab_w, tab_b, "table")
                    pe.wait_ge(st["ownout"], done("ownout", ph, b) - 1)
                    block_products(ps_b, feat, own_w, own_b, "own")
                    if ph == 3:
                        for a, c in HALF:
                            last = nc.tensor.matmul(ps_h[:, a:c], M["u_x"], feat[:, a:c], start=True, stop=True)
                        last.then_inc(st["upx"], 1)
                l = ph
                for k in ("feat", "tabout", "ownout") + (("upxout",) if ph == 3 else ()):
                    pe.wait_ge(st[k], done(k, ph, NB - 1))
                if ph in (1, 2):
                    pe.wait_ge(st["sum"], done("sum", ph, NB - 1))
                zero_visit(l)
                if l < 3:
                    with pe.Fori(0, SUPER) as j:
                        for s in range(RING):
                            agg_visits(l, j * RING + s, lambda k: rows_g[:, s, k, :],
                                       gathered[s], (l * SUPER + j + 1) * 16 * K)
                            signal(rows_used, ps_x[0:1, 0:1])
                    continue

                def edge_front(m, s):
                    pe.wait_ge(ea_in[s % 2], (m - s) * 8 + (s // 2) * 16 + 16)
                    pe.wait_ge(eat_made, m)
                    for k in range(K):
                        last = nc.tensor.transpose(ps_t[:, k * P:(k + 1) * P], ea[s % 2][:, k * P:(k + 1) * P], ident)
                    last.then_inc(turned, 1)

                def edge_back(m, s):
                    acc = ps_m[s % 2]
                    pe.wait_ge(m_sum, m + 1)
                    pe.wait_ge(eat_made, m + 1)
                    for k in range(K):
                        nc.tensor.matmul(acc[:, k * P:(k + 1) * P], eat[:, k * P:(k + 1) * P], M["m_edge"],
                                         start=(k % 4 == 0), stop=(k % 4 == 3), skip_group_check=True)
                    lo, hi = windows(pe, m)
                    with pe.Fori(lo, hi) as w:
                        q = pe.snap(qvisit, min_val=0, max_val=1 << 20)
                        pe.wait_ge(hot_t, q + 1)
                        for k in range(K):
                            for part in range(3):
                                last = nc.tensor.matmul(
                                    acc[:, k * P:(k + 1) * P], onehot_t[:, bass.ds(q % 2, 1), k * P:(k + 1) * P],
                                    q_parts[:, part, bass.ds(w * P, P)], start=False, stop=True, skip_group_check=True)
                        last.then_inc(q_added, 1)
                        pe.reg_add(qvisit, qvisit, 1)
                    signal(m_done, acc[0:1, GE - 1:GE], start=False)

                def edge_sum(a, s):
                    agg_visits(3, a, lambda k: msg[s % 2][:, k * P:(k + 1) * P], m_relu, a + 1 + RING)
                    signal(msg_used, ps_m[s % 2][0:1, 0:1])

                for m in range(RING):
                    edge_front(m, m)
                    if m >= 2:
                        edge_sum(m - 2, m - 2)
                    edge_back(m, m)
                with pe.Fori(1, SUPER) as j:
                    for s in range(RING):
                        m = j * RING + s
                        edge_front(m, s)
                        edge_sum(m - 2, s)
                        edge_back(m, s)
                for a in (NG - 2, NG - 1):
                    edge_sum(a, a % 2)

            with pe.Fori(0, NB) as b:
                pe.wait_ge(st["mean"], done("mean", 4, b))
                pe.wait_ge(st["aggd"], b)
                for a, c in HALF:
                    nc.tensor.matmul(ps_h[:, a:c], M["m_w2"], mean[:, a:c], start=True, stop=False)
                    last = nc.tensor.matmul(ps_h[:, a:c], R["m_b2"], ind[0:1, a:c], start=False, stop=True)
                last.then_inc(st["proj"], 1)
                pe.wait_ge(st["aggd"], b + 1)
                pe.wait_ge(st["usum"], b)
                for a, c in HALF:
                    last = nc.tensor.matmul(ps_t[:, a:c], M["u_agg"], zr[:, a:c], start=True, stop=True)
                last.then_inc(st["uagg"], 1)
                pe.wait_ge(st["urelu"], b + 1)
                pe.wait_ge(st["outsb"], b)
                block_products(ps_x, feat, "u_w2", "u_b2", "out")

        @block.scalar
        def _(act):
            act.wait_ge(in_const, 64)
            act.wait_ge(ready, 1)
            for ph in range(4):
                with act.Fori(0, NB) as b:
                    if ph in (1, 2):
                        act.wait_ge(st["sum"], done("sum", ph, b))
                        act.wait_ge(st["norm"], done("norm", ph, b) - 1)
                        nc.scalar.activation(zr, z, ACT.Relu).then_inc(st["relu"], 1)
                    act.wait_ge(st["stats"], done("stats", ph, b))
                    nc.scalar.activation(std[:, :], mv[:, :, 1], ACT.Sqrt, bias=eps[:, 0:1]).then_inc(st["std"], 1)
                    act.wait_ge(st["turn"], done("turn", ph, b))
                    act.wait_ge(st["own"], done("own", ph, b) - 1)
                    if ph == 3:
                        act.wait_ge(st["upx"], b)
                    if ph in (1, 2):
                        nc.scalar.activation(feat, ps_t[:, 0:BW], ACT.Identity, bias=C[f"b{ph - 1}"],
                                             scale=C[f"g{ph - 1}"]).then_inc(st["feat"], 1)
                    else:
                        nc.scalar.activation(feat, ps_t[:, 0:BW], ACT.Relu).then_inc(st["feat"], 1)
                    act.wait_ge(st["table"], done("table", ph, b))
                    act.wait_ge(tab_out, (ph * NB + b) * 16)
                    nc.scalar.activation(stage, ps_x[:, 0:BW], ACT.Relu if ph < 3 else ACT.Copy) \
                        .then_inc(st["tabout"], 1)
                    if ph == 3:
                        act.wait_ge(st["upx"], b + 1)
                        act.sem_inc(passed, 1)
                        nc.scalar.activation(blk(own, b), ps_h[:, 0:BW], ACT.Copy).then_inc(st["upxout"], 1)
            act.wait_ge(tab_out, 16 * NB * 4)
            act.wait_ge(st["sum"], done("sum", 3, NB - 1))
            with act.Fori(0, SUPER) as j:
                for s in range(RING):
                    m = j * RING + s
                    act.wait_ge(turned, m + 3)
                    act.wait_ge(m_done, m + 2)
                    nc.scalar.activation(eat, ps_t[:, :], ACT.Copy).then_inc(eat_made, 1)
                    act.wait_ge(m_sum, m + 3)
                    act.wait_ge(msg_used, m + 1)
                    nc.scalar.activation(msg[s % 2], rows_g[:, s, :, :].rearrange("p k f -> p (k f)"), ACT.Relu) \
                        .then_inc(m_relu, 1)
            with act.Fori(0, NB) as b:
                act.wait_ge(st["proj"], done("proj", 4, b))
                act.wait_ge(st["uagg"], b)
                nc.scalar.activation(zr, ps_h[:, 0:BW], ACT.Copy).then_inc(st["aggd"], 1)
                act.wait_ge(st["usum"], b + 1)
                act.wait_ge(st["out"], b)
                nc.scalar.activation(feat, y, ACT.Relu, bias=C["u_b1"]).then_inc(st["urelu"], 1)

        @block.vector
        def _(dve):
            links = [0]

            def link(ins):
                links[0] += 1
                ins.then_inc(chain, 1)
                dve.wait_ge(chain, links[0])

            visit = dve.alloc_register("dve_visit")
            qvisit = dve.alloc_register("dve_qvisit")
            prev = dve.alloc_register("dve_prev")
            dve.reg_mov(visit, 0)
            dve.reg_mov(qvisit, 0)
            dve.sem_inc(added, 2)
            dve.sem_inc(m_sum, 2)
            dve.memset(zeros[:, :], 0.0)
            dve.memset(ones_row[:, :], 1.0)
            dve.memset(ones[:, :], 1.0)
            dve.memset(eps[:, :], EPS).then_inc(ready, 1)
            dve.wait_ge(in_dstg, 16)
            dve.tensor_reduce(win_m[:, 0:1], dst_g_sb, AX.X, ALU.min)
            link(dve.tensor_reduce(win_m[:, 1:2], dst_g_sb, AX.X, ALU.max))
            link(dve.tensor_scalar(win_s[:, :], win_m[:, :], 7, None, ALU.arith_shift_right))
            dve.tensor_scalar(win_s[:, 1:2], win_s[:, 1:2], 1.0, None, ALU.add).then_inc(win_made, 1)
            dve.wait_ge(in_dst, 16)
            dve.tensor_copy(dst_f[:, :], dst_i[:, :])
            link(dve.memset(cnt[:, :], 0.0))
            dve.wait_ge(in_const, 64)
            dve.wait_ge(win_in, 16)

            for ph in range(5):
                ch = sem(f"chain{ph}")
                per = {0: 1, 1: 4, 2: 1, 3: 6, 4: 0}[ph]

                with dve.Fori(0, NB) as b:
                    step = [0]

                    def then(ins):
                        step[0] += 1
                        ins.then_inc(ch, 1)
                        dve.wait_ge(ch, b * per + step[0])

                    if ph:
                        dve.wait_ge(st["proj"], done("proj", ph, b) - 1)
                        c = blk(cnt, b)
                        if ph == 1:
                            dve.wait_ge(st["turn"], done("turn", 1, b) - 1)
                            then(dve.tensor_scalar(y, c, 1.0, None, ALU.max))
                            then(dve.reciprocal(y, y))
                            then(dve.scalar_tensor_tensor(c, c, 1.0, y, ALU.min, ALU.mult))
                        if ph == 4:
                            dve.tensor_scalar(ind, cnt[0:1, bass.ds(b * BW, BW)], 0.0, None, ALU.is_gt)
                        dve.tensor_tensor(mean, blk(agg, b), c, ALU.mult).then_inc(st["mean"], 1)
                    if ph == 4:
                        dve.wait_ge(st["uagg"], b + 1)
                        dve.wait_ge(st["urelu"], b)
                        dve.tensor_tensor(y, ps_t[:, 0:BW], blk(own, b), ALU.add).then_inc(st["usum"], 1)
                        dve.wait_ge(st["out"], b + 1)
                        dve.wait_ge(x_in, 16 * (2 * NB + 1 + b))
                        dve.wait_ge(final_out, 16 * b)
                        dve.tensor_tensor(stage, ps_x[:, 0:BW], extra, ALU.add).then_inc(st["outsb"], 1)
                        continue
                    src_z = zr if ph in (1, 2) else z
                    if ph:
                        dve.wait_ge(st["proj"], done("proj", ph, b))
                        if ph == 3:
                            dve.wait_ge(x1_out, 16 * b)
                            dve.wait_ge(x_in, 16 * (NB + 1 + b))
                            then(dve.tensor_tensor(z, ps_h[:, 0:BW], blk(own, b), ALU.add))
                            dve.tensor_tensor(z, z, extra, ALU.add).then_inc(st["sum"], 1)
                            dve.wait_ge(st["sum"], done("sum", ph, b))
                        else:
                            dve.tensor_tensor(z, ps_h[:, 0:BW], blk(own, b), ALU.add).then_inc(st["sum"], 1)
                            dve.wait_ge(st["relu"], done("relu", ph, b))
                    else:
                        dve.wait_ge(x_in, 16 * (b + 1))
                    for t in range(TB):
                        last = dve.bn_stats(st6[:, t, :], src_z[:, t * P:(t + 1) * P])
                    then(last)
                    dve.sem_inc(passed, 1)
                    for t in range(TB):
                        last = dve.bn_aggr(mv[:, t, :], st6[:, t, :])
                    last.then_inc(st["stats"], 1)
                    dve.wait_ge(st["stats"], done("stats", ph, b))
                    dve.wait_ge(st["std"], done("std", ph, b))
                    dve.reciprocal(rstd[:, :], std[:, :]).then_inc(st["rstd"], 1)
                    dve.wait_ge(st["rstd"], done("rstd", ph, b))
                    dve.wait_ge(st["turn"], done("turn", ph, b) - 1)
                    for t in range(TB):
                        last = dve.tensor_scalar(y[:, t * P:(t + 1) * P], src_z[:, t * P:(t + 1) * P],
                                                 mv[:, t, 0:1], rstd[:, t:t + 1], ALU.subtract, ALU.mult)
                    last.then_inc(st["norm"], 1)
                    dve.wait_ge(st["own"], done("own", ph, b))
                    if ph < 3:
                        dve.tensor_scalar(blk(own, b), ps_b[:, 0:BW], 1.0, None, ALU.mult).then_inc(st["ownout"], 1)
                    else:
                        part = [q_parts[:, i, bass.ds(b * BW, BW)] for i in range(3)]
                        then(dve.tensor_scalar(part[0], ps_b[:, 0:BW], 1.0, None, ALU.mult))
                        then(dve.tensor_tensor(zr, ps_b[:, 0:BW], part[0], ALU.subtract))
                        then(dve.tensor_scalar(part[1], zr, 1.0, None, ALU.mult))
                        then(dve.tensor_tensor(zr, zr, part[1], ALU.subtract))
                        dve.tensor_scalar(part[2], zr, 1.0, None, ALU.mult).then_inc(st["ownout"], 1)
                if ph == 4:
                    break
                l = ph
                dve.wait_ge(st["ownout"], done("ownout", ph, NB - 1))
                dve.reg_mov(prev, 0)
                dve.sem_inc(hot, 1)
                dve.reg_add(visit, visit, 1)
                link(dve.memset(agg[:, :], 0.0))

                def add_last(v):
                    dve.wait_ge(aggd, v + 2)
                    dve.wait_ge(added, v + 1)
                    at = dve.snap(prev, min_val=0, max_val=NPAD - P)
                    slot = bass.ds((v + 1) % 2, 1)
                    if l == 0:
                        c = cnt[:, bass.ds(at, P)].rearrange("p (a n) -> p a n", a=1)
                        dve.tensor_tensor(c, c, ps_c[:, slot, 0:P], ALU.add)
                    a = agg[:, bass.ds(at, P)].rearrange("p (a n) -> p a n", a=1)
                    dve.tensor_tensor(a, a, ps_a[:, slot, 0:P], ALU.add).then_inc(added, 1)

                def hot_visits(g):
                    lo, hi = windows(dve, g)
                    with dve.Fori(lo, hi) as w:
                        v = dve.snap(visit, min_val=1, max_val=1 << 20)
                        dve.wait_ge(aggd, v + 1)
                        dve.scalar_tensor_tensor(
                            onehot[:, bass.ds(v % 2, 1), :, :].rearrange("p s k n -> p (s k) n"),
                            con[:, C_IOTA:C_IOTA + P].rearrange("p (a n) -> p a n", a=1).broadcast_to([P, K, P]),
                            con[:, bass.ds(w + C_BASE, 1)],
                            dst_f[:, bass.ds(g * K, K)].rearrange("p (k a) -> p k a", a=1).broadcast_to([P, K, P]),
                            ALU.add, ALU.is_equal).then_inc(hot, 1)
                        add_last(v)
                        dve.reg_mov(prev, w * P)
                        dve.reg_add(visit, visit, 1)

                if l < 3:
                    with dve.Fori(0, NG) as g:
                        hot_visits(g)
                else:
                    def hot_t_visits(m, s):
                        dve.wait_ge(dt_in[s % 2], (m - s) * 8 + (s // 2) * 16 + 16)
                        lo, hi = windows(dve, m)
                        with dve.Fori(lo, hi) as w:
                            q = dve.snap(qvisit, min_val=0, max_val=1 << 20)
                            dve.wait_ge(q_added, q + 1)
                            dve.tensor_scalar(onehot_t[:, bass.ds(q % 2, 1), :],
                                              dtb[s % 2].rearrange("p (a e) -> p a e", a=1),
                                              con[:, bass.ds(w + C_NODE, 1)], None, ALU.is_equal).then_inc(hot_t, 1)
                            dve.reg_add(qvisit, qvisit, 1)
                        dve.wait_ge(m_done, m + 3)
                        dve.wait_ge(gathered[s], (m - s) * 32 + (3 * SUPER + 1) * 16 * K)
                        r = rows_g[:, s, :, :].rearrange("p k f -> p (k f)")
                        dve.tensor_tensor(r, ps_m[s % 2][:, :], r, ALU.add).then_inc(m_sum, 1)

                    for m in range(RING):
                        if m >= 2:
                            hot_visits(m - 2)
                        hot_t_visits(m, m)
                    with dve.Fori(1, SUPER) as j:
                        for s in range(RING):
                            hot_visits(j * RING + s - 2)
                            hot_t_visits(j * RING + s, s)
                    for a in (NG - 2, NG - 1):
                        hot_visits(a)
                v = dve.snap(visit, min_val=1, max_val=1 << 20)
                add_last(v)
                dve.wait_ge(added, v + 2)
                dve.sem_inc(pass_done, 1)


def kernel(x, src, dst, edge_attr_128, L0_gnn_lin_w, L0_gnn_lin_b, L0_gnn_linl_w, L0_gnn_linl_b, L0_gnn_linr_w,
           L0_gnn_ln_g, L0_gnn_ln_b, L1_gnn_msg_w1, L1_gnn_msg_b1, L1_gnn_msg_w2, L1_gnn_msg_b2,
           L1_gnn_upd_w1, L1_gnn_upd_b1, L1_gnn_upd_w2, L1_gnn_upd_b2):
    import concourse.bacc as bacc
    from concourse.bass_utils import run_bass_kernel_spmd

    def padded(a, n, fill=0):
        a = np.asarray(a)
        p = np.full((n,) + a.shape[1:], fill, a.dtype)
        p[:a.shape[0]] = a
        return p

    srcs = padded(src, EPAD).astype(np.int32).reshape(NG, P, K)
    dsts = padded(dst, EPAD, NPAD - 1).astype(np.int32).reshape(NG, P, K)
    by_edge = lambda a: np.ascontiguousarray(a.transpose(1, 0, 2)).reshape(P, NG * K)
    consts = np.zeros((P, C_END), np.float32)
    consts[:, C_IOTA:C_IOTA + P] = np.arange(P)
    consts[:, C_BASE:C_BASE + NT] = np.arange(NT) * P
    consts[:, C_NODE:C_NODE + NT] = np.arange(NT) * P + np.arange(P)[:, None]
    consts[:, C_ID:C_ID + P] = np.eye(P)
    lin, wl, wr = (np.asarray(a).transpose(0, 2, 1) for a in (L0_gnn_lin_w, L0_gnn_linl_w, L0_gnn_linr_w))
    w1, u1 = np.asarray(L1_gnn_msg_w1), np.asarray(L1_gnn_upd_w1)
    mats = [*lin, *wl, *wr, w1[:D], w1[D:2 * D], w1[2 * D:], np.asarray(L1_gnn_msg_w2),
            u1[:D], u1[D:], np.asarray(L1_gnn_upd_w2)]
    rows = [*np.asarray(L0_gnn_lin_b), *np.asarray(L0_gnn_linl_b), np.asarray(L1_gnn_msg_b1),
            np.asarray(L1_gnn_msg_b2), np.asarray(L1_gnn_upd_b2)]
    cols = [*np.asarray(L0_gnn_ln_g), *np.asarray(L0_gnn_ln_b), np.asarray(L1_gnn_upd_b1)]
    arrays = {
        "x": padded(x, NPAD),
        "src": by_edge(srcs),
        "dst": by_edge(dsts),
        "dst_t": np.ascontiguousarray(dsts.transpose(0, 2, 1)).reshape(NG, GE),
        "dst_g": np.ascontiguousarray(dsts.reshape(NG, GE)),
        "edge_attr": padded(edge_attr_128, EPAD),
        "consts": consts,
        "mats": np.ascontiguousarray(np.stack(mats, axis=1)),
        "rows": np.stack(rows)[None],
        "cols": np.ascontiguousarray(np.stack(cols, axis=1)),
    }
    nc = bacc.Bacc("TRN2", target_bir_lowering=False, num_devices=1)
    ins = [nc.dram_tensor(n, a.shape, mybir.dt.from_np(a.dtype), kind="ExternalInput").ap() for n, a in arrays.items()]
    out = nc.dram_tensor("out", (NPAD, D), F32, kind="ExternalOutput").ap()
    gnn_kernel(nc, *ins, out)
    r = run_bass_kernel_spmd(nc, [arrays], core_ids=[0])
    return r.results[0]["out"][:N]
```

```python
from contextlib import ExitStack

import numpy as np

import concourse.bass as bass
from concourse import mybir

N, D, E = 6250, 128, 106250
P = 128
NT = -(-N // P)
NPAD = NT * P
K = 8
GE = P * K
RING = 4
NG = RING * (-(-E // (GE * RING)))
EPAD = NG * GE
SUPER = NG // RING
TB = 7
NB = NT // TB
BW = TB * P
assert NB * TB == NT
EPS = 1e-5

F32, BF16, I32 = mybir.dt.float32, mybir.dt.bfloat16, mybir.dt.int32
ALU, ACT, AX = mybir.AluOpType, mybir.ActivationFunctionType, mybir.AxisListType

C_IOTA, C_BASE, C_NODE, C_ID, C_END = 0, P, P + NT, P + 2 * NT, 2 * P + 2 * NT

MATS = ["lin0", "lin1", "lin2", "wl0", "wl1", "wl2", "wr0", "wr1", "wr2",
        "m_src", "m_dst", "m_edge", "m_w2", "u_x", "u_agg", "u_w2"]
ROWS = ["lin_b0", "lin_b1", "lin_b2", "wl_b0", "wl_b1", "wl_b2", "m_b1", "m_b2", "u_b2"]
COLS = ["g0", "g1", "b0", "b1", "u_b1", "m_b2"]

TIMES = {0: NB, 1: NT, 2: NT, 3: NT, 4: NB}
STEPS = {
    "mean": (1, 2, 3, 4),
    "zeroed": (1, 2, 3),
    "proj": (1, 2, 3, 4),
    "sum": (1, 2, 3),
    "relu": (1, 2),
    "keep": (3,),
    "stats": (0, 1, 2, 3),
    "std": (0, 1, 2, 3),
    "rstd": (0, 1, 2, 3),
    "norm": (0, 1, 2, 3),
    "turn": (0, 1, 2, 3),
    "feat": (0, 1, 2, 3),
    "table": (0, 1, 2, 3),
    "tabadd": (0,),
    "tabout": (0, 1, 2, 3),
    "own": (0, 1, 2, 3),
    "ownout": (0, 1, 2, 3),
    "split": (3,),
    "upx": (3,),
    "upxout": (3,),
    "aggout": (4,),
    "uagg": (4,),
    "usum": (4,),
    "urelu": (4,),
    "out": (4,),
    "outsb": (4,),
}


def done(step, phase, i):
    return sum(TIMES[q] for q in STEPS[step] if q < phase) + i + 1


def gnn_kernel(nc, x, src, dst, dst_t, dst_g, edge_attr, consts, mats, rows, cols, out):
    ctx = ExitStack()
    with ctx:
        def sb(name, shape, dt=F32):
            return ctx.enter_context(nc.sbuf_tensor(name, shape, dt))

        def sem(name):
            return ctx.enter_context(nc.semaphore(name))

        tables = [nc.dram_tensor(f"table{i}", (NPAD, D), F32).ap() for i in range(2)]
        x1_dram = nc.dram_tensor("x1_dram", (NPAD, D), F32).ap()
        win_dram = nc.dram_tensor("win_dram", (NG, 2), I32).ap()

        con = sb("con", [P, C_END])
        mat = sb("mat", [P, len(MATS), D])
        row = sb("row", [P, len(ROWS), D])
        col = sb("col", [P, len(COLS)])
        ones_row = sb("ones_row", [1, P])
        ones = sb("ones", [P, P], BF16)
        zeros = sb("zeros", [P, P])
        eps = sb("eps", [P, 1])
        dst_i = sb("dst_i", [P, NG * K], I32)
        dst_f = sb("dst_f", [P, NG * K])
        win_m = sb("win_m", [NG, 2], I32)
        win_s = sb("win_s", [NG, 2], I32)
        win = sb("win", [1, NG, 4], I32)
        least = sb("least", [1, 2, 2 * P])

        agg = sb("agg", [P, NPAD])
        cnt = sb("cnt", [P, NPAD])
        own = sb("own", [P, NPAD])
        q_parts = sb("q_parts", [P, 3, NPAD], BF16)
        x_all = q_parts[:, 0:2, :].rearrange("p a n -> p (a n)").bitcast(F32)

        idx = sb("idx", [P, RING, K], I32)
        rows_g = sb("rows_g", [P, RING, K, D])
        onehot = sb("onehot", [P, 2, K, P])
        buf = sb("buf", [P, 8 * GE])
        dst_g_sb = buf[0:NG, 7 * GE:8 * GE].bitcast(I32)
        ea = [buf[:, i * GE:(i + 1) * GE] for i in range(2)]
        eat = buf[:, 2 * GE:3 * GE]
        dtb = [buf[:, i * GE:(i + 1) * GE].bitcast(I32) for i in (3, 4)]
        msg = [buf[:, i * GE:(i + 1) * GE] for i in (5, 6)]
        onehot_t = buf[:, 7 * GE:8 * GE].bitcast(BF16).rearrange("p (s e) -> p s e", s=2)
        mean_b, agg_b, y_b, feat_b, stage_b, res_b, ind_b = (buf[:, i * GE:i * GE + BW] for i in range(7))
        st6_b = sb("st6_b", [P, NT, 6])
        mv_b = sb("mv_b", [P, NT, 2])
        std_b = sb("std_b", [P, NT])
        rstd_b = sb("rstd_b", [P, NT])
        mean, z, zr, y, feat, stage, res, keep, rest, rest2 = (
            sb(n, [P, D]) for n in ("mean", "z", "zr", "y", "feat", "stage", "res", "keep", "rest", "rest2"))
        st6 = sb("st6", [P, 6])
        mv = sb("mv", [P, 2])
        std = sb("std", [P, 1])
        rstd = sb("rstd", [P, 1])

        def pb(name):
            return ctx.enter_context(nc.psum_tensor(name, [P, GE], F32))

        ps_h, ps_t, ps_x, ps_b = pb("ps_h"), pb("ps_t"), pb("ps_x"), pb("ps_b")
        ps_m = [ps_x, ps_b]
        ps_a = ps_h[:, :].rearrange("p (s c) -> p s c", s=2)
        ps_c = ps_t[:, :].rearrange("p (s c) -> p s c", s=2)
        tp_h, tp_t, tp_x, tp_b = ps_x[:, 0:D], ps_x[:, GE // 2:GE // 2 + D], ps_b[:, 0:D], ps_b[:, GE // 2:GE // 2 + D]

        in_const = sem("in_const")
        in_dst = sem("in_dst")
        in_dstg = sem("in_dstg")
        ready = sem("ready")
        win_made = sem("win_made")
        win_out = sem("win_out")
        win_in = sem("win_in")
        win_done = sem("win_done")
        st = {k: sem("n_" + k) for k in STEPS}
        chain = sem("chain")
        in_x = [sem(f"in_x{b}") for b in range(NB)]
        res_in = sem("res_in")
        tab_out = sem("tab_out")
        x1_out = sem("x1_out")
        final_out = sem("final_out")
        ind_made = sem("ind_made")
        idx_in = [sem(f"idx_in{s}") for s in range(RING)]
        gathered = [sem(f"gathered{s}") for s in range(RING)]
        passed = sem("passed")
        rows_used = sem("rows_used")
        hot = sem("hot")
        summed = sem("summed")
        added = sem("added")
        pass_done = sem("pass_done")
        ea_in = [sem("ea_in0"), sem("ea_in1")]
        dt_in = [sem("dt_in0"), sem("dt_in1")]
        turned = sem("turned")
        eat_made = sem("eat_made")
        hot_t = sem("hot_t")
        q_added = sem("q_added")
        m_done = sem("m_done")
        m_sum = sem("m_sum")
        m_relu = sem("m_relu")
        msg_used = sem("msg_used")

        M = {k: mat[:, i, :] for i, k in enumerate(MATS)}
        R = {k: row[0:1, i, :] for i, k in enumerate(ROWS)}
        RB = {k: row[:, i, :] for i, k in enumerate(ROWS)}
        C = {k: col[:, i:i + 1] for i, k in enumerate(COLS)}
        ident = con[:, C_ID:C_ID + P]

        def tile(t, i):
            return t[:, bass.ds(i * P, P)]

        def blk(t, b):
            return t[:, bass.ds(b * BW, BW)]

        def dram_blk(t, b):
            return t[bass.ds(b * BW, BW), :].rearrange("(t p) f -> p t f", p=P)

        def tiles(t):
            return t.rearrange("p (t f) -> p t f", f=P)

        def over_tiles(r):
            return r.rearrange("p (a f) -> p a f", a=1).broadcast_to([P, TB, D])

        class Windows:

            def __init__(self, eng, name):
                self.eng = eng
                self.now = [eng.alloc_register(f"{name}_win{i}") for i in range(4 * RING)]
                self.old = [eng.alloc_register(f"{name}_old{i}") for i in range(6)]
                self.tile = eng.alloc_register(f"{name}_tile")

            def start(self):
                for r in (*self.now[4 * (RING - 2):], self.tile):
                    self.eng.reg_mov(r, 0)

            def load(self, j):
                for i, r in enumerate(self.old):
                    self.eng.reg_mov(r, self.now[4 * (RING - 2 + i // 3) + i % 3])
                self.eng.load(self.now, win[0:1, bass.ds(j * RING, RING), :].rearrange("o g c -> o (g c)"))

            def regs(self, s):
                return self.now[4 * s:4 * s + 3] if s >= 0 else self.old[3 * (s + 2):3 * (s + 2) + 3]

            def of(self, s):
                lo, hi, _ = self.regs(s)
                return (self.eng.snap(lo, min_val=0, max_val=NT - 1), self.eng.snap(hi, min_val=1, max_val=NT))

            def at(self):
                return self.eng.snap(self.tile, min_val=0, max_val=NT - 1)

            def ready(self, s):
                return self.eng.snap(self.tile, min_val=0, max_val=NT) < \
                    self.eng.snap(self.regs(s)[2], min_val=0, max_val=NT)

            def next(self):
                self.eng.reg_add(self.tile, self.tile, 1)

        block = ctx.enter_context(nc.Block())

        @block.sync
        def _(sp):
            sp.dma_start(dst_g_sb, dst_g).then_inc(in_dstg, 16)
            for b in range(NB):
                sp.dma_start(tiles(blk(x_all, b)), dram_blk(x, b)).then_inc(in_x[b], 16)
            sp.dma_start(con[:, :], consts).then_inc(in_const, 16)
            sp.dma_start(mat[:, :, :], mats).then_inc(in_const, 16)
            sp.dma_start(row[:, :, :], rows.partition_broadcast(P)).then_inc(in_const, 16)
            sp.dma_start(col[:, :], cols).then_inc(in_const, 16)
            sp.dma_start(dst_i[:, :], dst).then_inc(in_dst, 16)
            sp.wait_ge(win_made, 1)
            sp.dma_start(win_dram, win_s[:, :]).then_inc(win_out, 16)
            sp.wait_ge(win_out, 16)
            sp.dma_start(win[:, :, 0:2], win_dram.rearrange("(o g) c -> o g c", o=1)).then_inc(win_in, 16)

            with sp.Fori(0, NB) as b:
                sp.wait_ge(st["tabout"], b + 1)
                sp.sem_inc(passed, 1)
                sp.dma_start(dram_blk(tables[0], b), tiles(stage_b)).then_inc(tab_out, 16)

            for l in range(4):
                if l == 3:
                    sp.wait_ge(tab_out, 16 * NB)
                with sp.Fori(0, SUPER) as j:
                    for s in range(RING):
                        g = j * RING + s
                        sp.wait_ge(gathered[s], (l * SUPER + j) * 16 * K)
                        sp.sem_inc(passed, 1)
                        sp.dma_start(idx[:, s, :], src[:, bass.ds(g * K, K)]).then_inc(idx_in[s], 16)
                        if l == 3:
                            sp.wait_ge(turned, g + 1)
                            sp.sem_inc(passed, 1)
                            sp.dma_start(ea[s % 2].rearrange("p (k f) -> p k f", f=D),
                                         edge_attr[bass.ds(g * GE, GE), :].rearrange("(p k) f -> p k f", k=K)) \
                                .then_inc(ea_in[s % 2], 16)
                            sp.wait_ge(m_done, g + 1)
                            sp.sem_inc(passed, 1)
                            sp.dma_start(dtb[s % 2], dst_t[bass.ds(g, 1), :].partition_broadcast(P)) \
                                .then_inc(dt_in[s % 2], 16)
            sp.wait_ge(pass_done, 1)
            sp.dma_start(tiles(res_b), dram_blk(x1_dram, 0)).then_inc(res_in, 16)
            with sp.Fori(0, NB - 1) as b:
                sp.wait_ge(st["outsb"], b + 1)
                sp.sem_inc(passed, 1)
                sp.dma_start(tiles(res_b), dram_blk(x1_dram, b + 1)).then_inc(res_in, 16)
                sp.dma_start(dram_blk(out, b), tiles(stage_b)).then_inc(final_out, 16)
            sp.wait_ge(st["outsb"], NB)
            sp.dma_start(dram_blk(out, NB - 1), tiles(stage_b)).then_inc(final_out, 16)
            sp.wait_ge(final_out, 16 * NB)

        @block.gpsimd
        def _(pool):
            pool.sem_inc(rows_used, RING)
            pool.sem_inc(m_relu, RING)
            for l in range(4):
                pool.wait_ge(tab_out, 16 * (NB + l * NT))
                if l == 3:
                    pool.wait_ge(rows_used, 3 * NG + RING)
                with pool.Fori(0, SUPER) as j:
                    for s in range(RING):
                        if l < 3:
                            pool.wait_ge(rows_used, (l * SUPER + j) * RING + s + 1)
                        else:
                            pool.wait_ge(m_relu, j * RING + s + 1)
                        pool.wait_ge(idx_in[s], (l * SUPER + j + 1) * 16)
                        pool.sem_inc(passed, 1)
                        for k in range(K):
                            pool.indirect_dma_start(
                                rows_g[:, s, k, :], None, tables[l % 2],
                                bass.IndirectOffsetOnAxis(ap=idx[:, s, k:k + 1], axis=0),
                            ).then_inc(gathered[s], 16)

        @block.tensor
        def _(pe):
            w = Windows(pe, "pe")
            visit = pe.alloc_register("pe_visit")
            qvisit = pe.alloc_register("pe_qvisit")
            pe.reg_mov(visit, 0)
            pe.reg_mov(qvisit, 0)
            for s in (summed, turned, q_added, m_done, msg_used):
                pe.sem_inc(s, 2)
            pe.wait_ge(in_const, 64)
            pe.wait_ge(ready, 1)

            def signal(s, at, start=True):
                nc.tensor.matmul(at, zeros[0:1, 0:1], zeros[0:1, 0:1], start=start, stop=True,
                                 skip_group_check=not start).then_inc(s, 1)

            def zero_visit(l):
                v = pe.snap(visit, min_val=0, max_val=1 << 20)
                pe.wait_ge(added, v + 1)
                if l == 0:
                    nc.tensor.matmul(ps_c[:, bass.ds(v % 2, 1), 0:P], zeros[:, :], zeros[:, :], start=True, stop=True)
                nc.tensor.matmul(ps_a[:, bass.ds(v % 2, 1), 0:P], zeros[:, :], zeros[:, :],
                                 start=True, stop=True).then_inc(summed, 1)
                pe.reg_add(visit, visit, 1)

            def sum_visits(l, window, rows_of, rows_sem, rows_value):
                pe.wait_ge(rows_sem, rows_value)
                pe.sem_inc(passed, 1)
                with pe.Fori(*window):
                    v = pe.snap(visit, min_val=0, max_val=1 << 20)
                    pe.wait_ge(hot, v + 1)
                    pe.wait_ge(added, v + 1)
                    hs = onehot[:, bass.ds(v % 2, 1), :, :]
                    if l == 0:
                        halves = hs.bitcast(BF16).rearrange("p s k (n h) -> p s k n h", h=2)[:, :, :, :, 1]
                        for k in range(K):
                            nc.tensor.matmul(ps_c[:, bass.ds(v % 2, 1), 0:P], ones[:, :], halves[:, :, k, :],
                                             start=(k == 0), stop=(k == K - 1))
                    for k in range(K):
                        last = nc.tensor.matmul(ps_a[:, bass.ds(v % 2, 1), 0:P], rows_of(k), hs[:, :, k, :],
                                                start=(k == 0), stop=(k == K - 1))
                    last.then_inc(summed, 1)
                    pe.reg_add(visit, visit, 1)

            def block_products(dst_ps, lhs, rhs, s):
                for t in range(TB):
                    last = nc.tensor.matmul(dst_ps[:, t * P:(t + 1) * P], lhs[:, t * P:(t + 1) * P], M[rhs],
                                            start=True, stop=True)
                last.then_inc(st[s], 1)

            HALF = [(0, 512), (512, BW)]

            def turn_block(b):
                pe.wait_ge(st["norm"], done("norm", 0, b))
                if not (isinstance(b, int) and b == 0):
                    pe.wait_ge(st["feat"], done("feat", 0, b - 1))
                for t in range(TB):
                    last = nc.tensor.transpose(ps_t[:, t * P:(t + 1) * P], y_b[:, t * P:(t + 1) * P], ident)
                last.then_inc(st["turn"], 1)

            def project_block(b):
                pe.wait_ge(st["feat"], done("feat", 0, b))
                pe.wait_ge(st["tabadd"], b)
                block_products(ps_x, feat_b, "lin0", "table")
                pe.wait_ge(st["ownout"], b)
                block_products(ps_b, feat_b, "wr0", "own")

            turn_block(0)
            with pe.Fori(0, NB - 1) as b:
                turn_block(b + 1)
                project_block(b)
            project_block(NB - 1)
            for k in ("feat", "tabadd", "ownout"):
                pe.wait_ge(st[k], NB)

            def node_front(ph, t):
                pe.wait_ge(st["mean"], done("mean", ph, t))
                pe.wait_ge(st["sum"], done("sum", ph, t) - 1)
                if ph == 3:
                    pe.wait_ge(st["upxout"], t)
                nc.tensor.matmul(tp_h, mean[:, :], M[f"wl{ph - 1}"], start=True, stop=True).then_inc(st["proj"], 1)

            def node_back(ph, t):
                pe.wait_ge(st["norm"], done("norm", ph, t))
                pe.wait_ge(st["feat"], done("feat", ph, t) - 1)
                nc.tensor.transpose(tp_t, y[:, :], ident).then_inc(st["turn"], 1)
                pe.wait_ge(st["feat"], done("feat", ph, t))
                pe.wait_ge(st["tabout"], done("tabout", ph, t) - 1)
                if ph < 3:
                    nc.tensor.matmul(tp_x, feat[:, :], M[f"lin{ph}"], start=True, stop=False)
                    nc.tensor.matmul(tp_x, ones_row[0:1, :], R[f"lin_b{ph}"], start=False, stop=True) \
                        .then_inc(st["table"], 1)
                else:
                    nc.tensor.matmul(tp_x, feat[:, :], M["m_src"], start=True, stop=True).then_inc(st["table"], 1)
                pe.wait_ge(st["ownout"], done("ownout", ph, t) - 1)
                nc.tensor.matmul(tp_b, feat[:, :], M[f"wr{ph}" if ph < 3 else "m_dst"], start=True, stop=False)
                nc.tensor.matmul(tp_b, ones_row[0:1, :], R[f"wl_b{ph}" if ph < 3 else "m_b1"], start=False, stop=True) \
                    .then_inc(st["own"], 1)
                if ph == 3:
                    nc.tensor.matmul(tp_h, M["u_x"], feat[:, :], start=True, stop=True).then_inc(st["upx"], 1)

            pe.wait_ge(win_done, 1)
            zero_visit(0)
            for l in range(3):
                w.start()
                with pe.Fori(0, SUPER) as j:
                    w.load(j)
                    for s in range(RING):
                        with pe.If(w.ready(s - 2)):
                            node_front(l + 1, w.at())
                        sum_visits(l, w.of(s), lambda k: rows_g[:, s, k, :],
                                   gathered[s], (l * SUPER + j + 1) * 16 * K)
                        pe.drain().then_inc(rows_used, 1)
                        with pe.If(w.ready(s - 2)):
                            node_back(l + 1, w.at())
                            w.next()
                zero_visit(l)
                with pe.Fori(w.at(), NT) as t:
                    node_front(l + 1, t)
                    node_back(l + 1, t)

            pe.wait_ge(st["split"], NT + 1)
            for k in ("feat", "tabout", "ownout", "upxout"):
                pe.wait_ge(st[k], done(k, 3, NT - 1))

            def edge_front(m, s):
                pe.wait_ge(ea_in[s % 2], (m - s) * 8 + (s // 2) * 16 + 16)
                pe.wait_ge(eat_made, m)
                for k in range(K):
                    last = nc.tensor.transpose(ps_t[:, k * P:(k + 1) * P], ea[s % 2][:, k * P:(k + 1) * P], ident)
                last.then_inc(turned, 1)

            def edge_back(m, s):
                acc = ps_m[s % 2]
                pe.wait_ge(m_sum, m + 1)
                pe.wait_ge(eat_made, m + 1)
                for k in range(K):
                    nc.tensor.matmul(acc[:, k * P:(k + 1) * P], eat[:, k * P:(k + 1) * P], M["m_edge"],
                                     start=(k % 4 == 0), stop=(k % 4 == 3), skip_group_check=True)
                with pe.Fori(*w.of(s)) as n:
                    q = pe.snap(qvisit, min_val=0, max_val=1 << 20)
                    pe.wait_ge(hot_t, q + 1)
                    for k in range(K):
                        for part in range(3):
                            last = nc.tensor.matmul(
                                acc[:, k * P:(k + 1) * P], onehot_t[:, bass.ds(q % 2, 1), k * P:(k + 1) * P],
                                q_parts[:, part, bass.ds(n * P, P)], start=False, stop=True, skip_group_check=True)
                    last.then_inc(q_added, 1)
                    pe.reg_add(qvisit, qvisit, 1)
                signal(m_done, acc[0:1, GE - 1:GE], start=False)

            def edge_sum(a, s):
                sum_visits(3, w.of(s - 2), lambda k: msg[s % 2][:, k * P:(k + 1) * P], m_relu, a + 1 + RING)
                signal(msg_used, ps_m[s % 2][0:1, 0:1])

            w.load(0)
            for m in range(RING):
                edge_front(m, m)
                if m >= 2:
                    edge_sum(m - 2, m)
                edge_back(m, m)
            with pe.Fori(1, SUPER) as j:
                w.load(j)
                for s in range(RING):
                    edge_front(j * RING + s, s)
                    edge_sum(j * RING + s - 2, s)
                    edge_back(j * RING + s, s)
            for s in range(2):
                sum_visits(3, w.of(RING - 2 + s), lambda k: msg[s % 2][:, k * P:(k + 1) * P],
                           m_relu, NG - 2 + s + 1 + RING)

            def update_products(b):
                if not isinstance(b, int) or b + 1 < NB:
                    pe.wait_ge(st["mean"], done("mean", 4, b + 1))
                    pe.wait_ge(st["aggout"], b + 1)
                    for a, c in HALF:
                        last = nc.tensor.matmul(ps_h[:, a:c], M["m_w2"], mean_b[:, a:c], start=True, stop=True)
                    last.then_inc(st["proj"], 1)
                if not isinstance(b, int) or 0 <= b < NB:
                    pe.wait_ge(st["aggout"], b + 1)
                    pe.wait_ge(st["usum"], b)
                    for a, c in HALF:
                        last = nc.tensor.matmul(ps_t[:, a:c], M["u_agg"], agg_b[:, a:c], start=True, stop=True)
                    last.then_inc(st["uagg"], 1)
                if not isinstance(b, int) or 1 <= b:
                    pe.wait_ge(st["urelu"], b)
                    pe.wait_ge(st["outsb"], b - 1)
                    block_products(ps_x, feat_b, "u_w2", "out")

            pe.wait_ge(m_sum, NG + 2)
            for b in (-1, 0):
                update_products(b)
            with pe.Fori(1, NB - 1) as b:
                update_products(b)
            for b in (NB - 1, NB):
                update_products(b)

        @block.scalar
        def _(act):
            w = Windows(act, "act")
            act.wait_ge(in_const, 64)
            act.wait_ge(ready, 1)

            act.wait_ge(st["stats"], NB)
            nc.scalar.activation(std_b[:, :], mv_b[:, :, 1], ACT.Sqrt, bias=eps[:, 0:1]).then_inc(st["std"], NB)

            def feat_block(b):
                act.wait_ge(st["turn"], b + 1)
                act.wait_ge(st["own"], b)
                nc.scalar.activation(feat_b, ps_t[:, 0:BW], ACT.Relu).then_inc(st["feat"], 1)

            def table_block(b):
                act.wait_ge(st["tabadd"], b + 1)
                act.wait_ge(tab_out, b * 16)
                nc.scalar.activation(stage_b, agg_b, ACT.Relu).then_inc(st["tabout"], 1)

            feat_block(0)
            with act.Fori(0, NB - 1) as b:
                table_block(b)
                feat_block(b + 1)
            table_block(NB - 1)

            def node_tile(ph, t):
                def rows_of(dram):
                    return dram[bass.ds(t * P, P), :]

                if ph == 3:
                    act.wait_ge(st["sum"], done("sum", 3, t) - 1)
                    act.dma_start(res[:, :], rows_of(x)).then_inc(res_in, 16)
                act.wait_ge(st["stats"], done("stats", ph, t))
                nc.scalar.activation(std[:, :], mv[:, 1:2], ACT.Sqrt, bias=eps[:, 0:1]).then_inc(st["std"], 1)
                if ph == 3:
                    act.wait_ge(st["keep"], t + 1)
                    act.dma_start(rows_of(x1_dram), keep[:, :]).then_inc(x1_out, 16)
                act.wait_ge(st["turn"], done("turn", ph, t))
                act.wait_ge(st["own"], done("own", ph, t) - 1)
                if ph == 3:
                    act.wait_ge(st["upx"], t)
                    nc.scalar.activation(feat[:, :], tp_t, ACT.Relu).then_inc(st["feat"], 1)
                else:
                    nc.scalar.activation(feat[:, :], tp_t, ACT.Identity, bias=C[f"b{ph - 1}"],
                                         scale=C[f"g{ph - 1}"]).then_inc(st["feat"], 1)
                act.wait_ge(st["table"], done("table", ph, t))
                act.wait_ge(tab_out, (NB + (ph - 1) * NT + t) * 16)
                nc.scalar.activation(stage[:, :], tp_x, ACT.Relu if ph < 3 else ACT.Copy).then_inc(st["tabout"], 1)
                act.wait_ge(st["tabout"], done("tabout", ph, t))
                act.dma_start(rows_of(tables[ph % 2]), stage[:, :]).then_inc(tab_out, 16)
                act.wait_ge(st["own"], done("own", ph, t))
                if ph < 3:
                    act.wait_ge(st["sum"], done("sum", ph, t))
                    act.sem_inc(passed, 1)
                    nc.scalar.activation(tile(own, t), tp_b, ACT.Copy).then_inc(st["ownout"], 1)
                else:
                    act.wait_ge(st["split"], t)
                    nc.scalar.activation(rest[:, :], tp_b, ACT.Copy).then_inc(st["ownout"], 1)
                    act.wait_ge(st["upx"], t + 1)
                    act.sem_inc(passed, 1)
                    nc.scalar.activation(tile(own, t), tp_h, ACT.Copy).then_inc(st["upxout"], 1)

            act.wait_ge(win_done, 1)
            for l in range(3):
                w.start()
                with act.Fori(0, SUPER) as j:
                    w.load(j)
                    for s in range(RING):
                        with act.If(w.ready(s - 2)):
                            node_tile(l + 1, w.at())
                            w.next()
                with act.Fori(w.at(), NT) as t:
                    node_tile(l + 1, t)

            def eat_group(m):
                act.wait_ge(turned, m + 3)
                act.wait_ge(m_done, m + 2)
                nc.scalar.activation(eat, ps_t[:, :], ACT.Copy).then_inc(eat_made, 1)

            def relu_group(m, s):
                act.wait_ge(m_sum, m + 3)
                act.wait_ge(msg_used, m + 1)
                nc.scalar.activation(msg[s % 2], rows_g[:, s, :, :].rearrange("p k f -> p (k f)"), ACT.Relu) \
                    .then_inc(m_relu, 1)

            eat_group(0)
            with act.Fori(0, SUPER - 1) as j:
                for s in range(RING):
                    eat_group(j * RING + s + 1)
                    relu_group(j * RING + s, s)
            for s in range(RING):
                if s < RING - 1:
                    eat_group(NG - RING + s + 1)
                relu_group(NG - RING + s, s)

            with act.Fori(0, NB) as b:
                act.wait_ge(st["usum"], b + 1)
                act.wait_ge(st["out"], b)
                nc.scalar.activation(feat_b, y_b, ACT.Relu, bias=C["u_b1"]).then_inc(st["urelu"], 1)

        @block.vector
        def _(dve):
            w = Windows(dve, "dve")
            links = [0]

            def link(ins):
                links[0] += 1
                ins.then_inc(chain, 1)
                dve.wait_ge(chain, links[0])

            visit = dve.alloc_register("dve_visit")
            qvisit = dve.alloc_register("dve_qvisit")
            prev = dve.alloc_register("dve_prev")
            for r in (visit, qvisit, prev):
                dve.reg_mov(r, 0)
            dve.sem_inc(added, 2)
            dve.sem_inc(m_sum, 2)
            dve.memset(zeros[:, :], 0.0)
            dve.memset(ones_row[:, :], 1.0)
            dve.memset(ones[:, :], 1.0)
            dve.memset(rest[:, :], 0.0)
            dve.memset(win[:, :, :], 0)
            dve.memset(least[:, :, :], float(NT))
            dve.memset(eps[:, :], EPS).then_inc(ready, 1)
            dve.wait_ge(in_dstg, 16)
            dve.tensor_reduce(win_m[:, 0:1], dst_g_sb, AX.X, ALU.min)
            link(dve.tensor_reduce(win_m[:, 1:2], dst_g_sb, AX.X, ALU.max))
            link(dve.tensor_scalar(win_s[:, :], win_m[:, :], 7, None, ALU.arith_shift_right))
            dve.tensor_scalar(win_s[:, 1:2], win_s[:, 1:2], 1.0, None, ALU.add).then_inc(win_made, 1)

            for b in range(NB):
                dve.wait_ge(in_x[b], 16)
                for t in range(b * TB, (b + 1) * TB):
                    last = dve.bn_stats(st6_b[:, t, :], x_all[:, t * P:(t + 1) * P])
                link(last)
                for t in range(b * TB, (b + 1) * TB):
                    last = dve.bn_aggr(mv_b[:, t, :], st6_b[:, t, :])
                last.then_inc(st["stats"], 1)
            dve.wait_ge(st["std"], NB)
            dve.reciprocal(rstd_b[:, :], std_b[:, :]).then_inc(st["rstd"], NB)
            dve.wait_ge(st["rstd"], NB)
            dve.wait_ge(st["stats"], NB)
            dve.wait_ge(in_const, 64)

            def norm_block(b):
                if not (isinstance(b, int) and b == 0):
                    dve.wait_ge(st["turn"], b)
                for t in range(TB):
                    at = b * TB + t
                    last = dve.tensor_scalar(y_b[:, t * P:(t + 1) * P], tile(x_all, at),
                                             mv_b[:, bass.ds(at, 1), 0], rstd_b[:, bass.ds(at, 1)],
                                             ALU.subtract, ALU.mult)
                last.then_inc(st["norm"], 1)

            def out_block(b):
                dve.wait_ge(st["table"], b + 1)
                dve.wait_ge(st["tabout"], b)
                dve.tensor_tensor(tiles(agg_b), tiles(ps_x[:, 0:BW]), over_tiles(RB["lin_b0"]), ALU.add) \
                    .then_inc(st["tabadd"], 1)
                dve.wait_ge(st["own"], b + 1)
                dve.tensor_tensor(tiles(blk(own, b)), tiles(ps_b[:, 0:BW]), over_tiles(RB["wl_b0"]), ALU.add) \
                    .then_inc(st["ownout"], 1)

            norm_block(0)
            norm_block(1)
            with dve.Fori(0, NB - 2) as b:
                out_block(b)
                norm_block(b + 2)
            for b in (NB - 2, NB - 1):
                out_block(b)

            dve.wait_ge(win_in, 16)
            link(dve.tensor_copy(least[:, 0, 0:NG - 1], win[:, 1:NG, 0]))
            step, at = 1, 0
            while step < NG:
                link(dve.tensor_tensor(least[:, 1 - at, 0:P], least[:, at, 0:P], least[:, at, step:step + P], ALU.min))
                step, at = 2 * step, 1 - at
            dve.tensor_copy(win[:, :, 2], least[:, at, 0:NG]).then_inc(win_done, 1)
            dve.wait_ge(win_done, 1)
            dve.wait_ge(in_dst, 16)
            dve.tensor_copy(dst_f[:, :], dst_i[:, :])
            dve.memset(cnt[:, :], 0.0)
            link(dve.memset(agg[:, :], 0.0))

            def add_last(l, v):
                dve.wait_ge(summed, v + 2)
                dve.wait_ge(added, v + 1)
                at = dve.snap(prev, min_val=0, max_val=NPAD - P)
                slot = bass.ds((v + 1) % 2, 1)
                if l == 0:
                    c = cnt[:, bass.ds(at, P)].rearrange("p (a n) -> p a n", a=1)
                    dve.tensor_tensor(c, c, ps_c[:, slot, 0:P], ALU.add)
                a = agg[:, bass.ds(at, P)].rearrange("p (a n) -> p a n", a=1)
                dve.tensor_tensor(a, a, ps_a[:, slot, 0:P], ALU.add).then_inc(added, 1)

            def hot_visits(l, window, g):
                with dve.Fori(*window) as n:
                    v = dve.snap(visit, min_val=1, max_val=1 << 20)
                    dve.wait_ge(summed, v + 1)
                    dve.scalar_tensor_tensor(
                        onehot[:, bass.ds(v % 2, 1), :, :].rearrange("p s k n -> p (s k) n"),
                        con[:, C_IOTA:C_IOTA + P].rearrange("p (a n) -> p a n", a=1).broadcast_to([P, K, P]),
                        con[:, bass.ds(n + C_BASE, 1)],
                        dst_f[:, bass.ds(g * K, K)].rearrange("p (k a) -> p k a", a=1).broadcast_to([P, K, P]),
                        ALU.add, ALU.is_equal).then_inc(hot, 1)
                    add_last(l, v)
                    dve.reg_mov(prev, n * P)
                    dve.reg_add(visit, visit, 1)

            def zero_visit():
                dve.sem_inc(hot, 1)
                dve.reg_mov(prev, 0)
                dve.reg_add(visit, visit, 1)

            PER = {1: 3, 2: 1, 3: 5}
            within = {ph: sem(f"within{ph}") for ph in PER}

            def links_of(ph, t, before):
                step = [before]

                def then(ins):
                    step[0] += 1
                    ins.then_inc(within[ph], 1)
                    dve.wait_ge(within[ph], t * PER[ph] + step[0])
                return then

            def split(t, then):
                part = [q_parts[:, i, bass.ds(t, P)] for i in range(3)]
                then(dve.tensor_scalar(part[0], rest[:, :], 1.0, None, ALU.mult))
                then(dve.tensor_tensor(rest2[:, :], rest[:, :], part[0], ALU.subtract))
                then(dve.tensor_scalar(part[1], rest2[:, :], 1.0, None, ALU.mult))
                dve.tensor_tensor(part[2], rest2[:, :], part[1], ALU.subtract).then_inc(st["split"], 1)

            last_tile = dve.alloc_register("dve_last_tile")
            dve.reg_mov(last_tile, 0)

            def node_front(ph, t):
                then = links_of(ph, t, 0)
                c = tile(cnt, t)
                if ph == 1:
                    then(dve.tensor_scalar(c, c, 0.5, None, ALU.max))
                    dve.sem_inc(passed, 1)
                    then(dve.reciprocal(c, c))
                dve.wait_ge(st["proj"], done("proj", ph, t) - 1)
                dve.tensor_tensor(mean[:, :], tile(agg, t), c, ALU.mult).then_inc(st["mean"], 1)
                dve.wait_ge(st["mean"], done("mean", ph, t))
                dve.tensor_scalar(tile(agg, t), zeros[:, :], 0.0, None, ALU.add).then_inc(st["zeroed"], 1)
                if ph == 3:
                    dve.wait_ge(st["ownout"], done("ownout", 3, t) - 1)
                    at = dve.snap(last_tile, min_val=0, max_val=NPAD - P)
                    split(at, then)
                    dve.reg_mov(last_tile, t * P)

            def node_back(ph, t):
                then = links_of(ph, t, {1: 2, 2: 0, 3: 3}[ph])
                dve.wait_ge(st["proj"], done("proj", ph, t))
                if ph == 3:
                    dve.wait_ge(res_in, 16 * (t + 1))
                    then(dve.tensor_tensor(z[:, :], tp_h, tile(own, t), ALU.add))
                    dve.tensor_tensor(z[:, :], z[:, :], res[:, :], ALU.add).then_inc(st["sum"], 1)
                    dve.wait_ge(st["sum"], done("sum", ph, t))
                else:
                    dve.tensor_tensor(z[:, :], tp_h, tile(own, t), ALU.add).then_inc(st["sum"], 1)
                    dve.wait_ge(st["sum"], done("sum", ph, t))
                    dve.tensor_scalar(zr[:, :], z[:, :], 0.0, None, ALU.max).then_inc(st["relu"], 1)
                    dve.wait_ge(st["relu"], done("relu", ph, t))
                zz = z if ph == 3 else zr
                then(dve.bn_stats(st6[:, :], zz[:, :]))
                dve.sem_inc(passed, 1)
                dve.bn_aggr(mv[:, :], st6[:, :]).then_inc(st["stats"], 1)
                dve.wait_ge(st["stats"], done("stats", ph, t))
                if ph == 3:
                    dve.wait_ge(x1_out, 16 * t)
                    dve.tensor_tensor(keep[:, :], z[:, :], RB["u_b2"], ALU.add).then_inc(st["keep"], 1)
                dve.wait_ge(st["std"], done("std", ph, t))
                dve.reciprocal(rstd[:, :], std[:, :]).then_inc(st["rstd"], 1)
                dve.wait_ge(st["rstd"], done("rstd", ph, t))
                dve.wait_ge(st["turn"], done("turn", ph, t) - 1)
                dve.tensor_scalar(y[:, :], zz[:, :], mv[:, 0:1], rstd[:, 0:1], ALU.subtract, ALU.mult) \
                    .then_inc(st["norm"], 1)

            zero_visit()
            for l in range(3):
                w.start()
                dve.wait_ge(st["ownout"], NB + l * NT)
                with dve.Fori(0, SUPER) as j:
                    w.load(j)
                    for s in range(RING):
                        with dve.If(w.ready(s - 2)):
                            node_front(l + 1, w.at())
                        hot_visits(l, w.of(s), j * RING + s)
                        with dve.If(w.ready(s - 2)):
                            node_back(l + 1, w.at())
                            w.next()
                v = dve.snap(visit, min_val=1, max_val=1 << 20)
                add_last(l, v)
                dve.wait_ge(added, v + 2)
                zero_visit()
                with dve.Fori(w.at(), NT) as t:
                    node_front(l + 1, t)
                    node_back(l + 1, t)
                dve.wait_ge(st["zeroed"], (l + 1) * NT)

            dve.wait_ge(st["ownout"], done("ownout", 3, NT - 1))
            dve.wait_ge(st["split"], NT)
            split((NT - 1) * P, link)

            def hot_t_visits(m, s):
                dve.wait_ge(dt_in[s % 2], (m - s) * 8 + (s // 2) * 16 + 16)
                dve.sem_inc(passed, 1)
                with dve.Fori(*w.of(s)) as n:
                    q = dve.snap(qvisit, min_val=0, max_val=1 << 20)
                    dve.wait_ge(q_added, q + 1)
                    dve.tensor_scalar(onehot_t[:, bass.ds(q % 2, 1), :],
                                      dtb[s % 2].rearrange("p (a e) -> p a e", a=1),
                                      con[:, bass.ds(n + C_NODE, 1)], None, ALU.is_equal).then_inc(hot_t, 1)
                    dve.reg_add(qvisit, qvisit, 1)

            def add_rows(m, s):
                dve.wait_ge(m_done, m + 3)
                dve.wait_ge(gathered[s], (m - s) * 32 + (3 * SUPER + 1) * 16 * K)
                r = rows_g[:, s, :, :].rearrange("p k f -> p (k f)")
                dve.tensor_tensor(r, ps_m[s % 2][:, :], r, ALU.add).then_inc(m_sum, 1)

            w.load(0)
            for m in range(RING):
                hot_t_visits(m, m)
                if m >= 1:
                    hot_visits(3, w.of(m - 1), m - 1)
                add_rows(m, m)
            with dve.Fori(1, SUPER) as j:
                w.load(j)
                for s in range(RING):
                    hot_t_visits(j * RING + s, s)
                    hot_visits(3, w.of(s - 1), j * RING + s - 1)
                    add_rows(j * RING + s, s)
            hot_visits(3, w.of(RING - 1), NG - 1)
            v = dve.snap(visit, min_val=1, max_val=1 << 20)
            add_last(3, v)
            dve.wait_ge(added, v + 2)
            dve.sem_inc(pass_done, 1)

            def means(b):
                if not (isinstance(b, int) and b == 0):
                    dve.wait_ge(st["proj"], done("proj", 4, b - 1))
                dve.tensor_tensor(mean_b, blk(agg, b), blk(cnt, b), ALU.mult).then_inc(st["mean"], 1)
                if not (isinstance(b, int) and b == 0):
                    dve.wait_ge(st["aggout"], b)
                dve.tensor_scalar(ind_b, blk(cnt, b), 1.5, C["m_b2"], ALU.is_lt, ALU.mult).then_inc(ind_made, 1)

            def update_sums(b):
                if not isinstance(b, int) or b + 1 < NB:
                    dve.wait_ge(st["proj"], done("proj", 4, b + 1))
                    dve.wait_ge(ind_made, b + 2)
                    if not isinstance(b, int) or b >= 0:
                        dve.wait_ge(st["uagg"], b + 1)
                    dve.tensor_tensor(agg_b, ps_h[:, 0:BW], ind_b, ALU.add).then_inc(st["aggout"], 1)
                if not isinstance(b, int) or 0 <= b < NB:
                    dve.wait_ge(st["uagg"], b + 1)
                    dve.wait_ge(st["urelu"], b)
                    dve.tensor_tensor(y_b, ps_t[:, 0:BW], blk(own, b), ALU.add).then_inc(st["usum"], 1)
                if not isinstance(b, int) or b >= 1:
                    dve.wait_ge(st["out"], b)
                    dve.wait_ge(res_in, 16 * (NT + b))
                    dve.wait_ge(final_out, 16 * (b - 1))
                    dve.tensor_tensor(stage_b, ps_x[:, 0:BW], res_b, ALU.add).then_inc(st["outsb"], 1)
                if not isinstance(b, int) or b + 2 < NB:
                    means(b + 2)

            dve.wait_ge(st["upxout"], NT)
            means(0)
            for b in (-1, 0):
                update_sums(b)
            with dve.Fori(1, NB - 2) as b:
                update_sums(b)
            for b in (NB - 2, NB - 1, NB):
                update_sums(b)


def kernel(x, src, dst, edge_attr_128, L0_gnn_lin_w, L0_gnn_lin_b, L0_gnn_linl_w, L0_gnn_linl_b, L0_gnn_linr_w,
           L0_gnn_ln_g, L0_gnn_ln_b, L1_gnn_msg_w1, L1_gnn_msg_b1, L1_gnn_msg_w2, L1_gnn_msg_b2,
           L1_gnn_upd_w1, L1_gnn_upd_b1, L1_gnn_upd_w2, L1_gnn_upd_b2):
    import concourse.bacc as bacc
    from concourse.bass_utils import run_bass_kernel_spmd

    def padded(a, n, fill=0):
        a = np.asarray(a)
        p = np.full((n,) + a.shape[1:], fill, a.dtype)
        p[:a.shape[0]] = a
        return p

    srcs = padded(src, EPAD).astype(np.int32).reshape(NG, P, K)
    dsts = padded(dst, EPAD, NPAD - 1).astype(np.int32).reshape(NG, P, K)
    by_edge = lambda a: np.ascontiguousarray(a.transpose(1, 0, 2)).reshape(P, NG * K)
    consts = np.zeros((P, C_END), np.float32)
    consts[:, C_IOTA:C_IOTA + P] = np.arange(P)
    consts[:, C_BASE:C_BASE + NT] = np.arange(NT) * P
    consts[:, C_NODE:C_NODE + NT] = np.arange(NT) * P + np.arange(P)[:, None]
    consts[:, C_ID:C_ID + P] = np.eye(P)
    lin, wl, wr = (np.asarray(a).transpose(0, 2, 1) for a in (L0_gnn_lin_w, L0_gnn_linl_w, L0_gnn_linr_w))
    w1, u1 = np.asarray(L1_gnn_msg_w1), np.asarray(L1_gnn_upd_w1)
    mats = [*lin, *wl, *wr, w1[:D], w1[D:2 * D], w1[2 * D:], np.asarray(L1_gnn_msg_w2),
            u1[:D], u1[D:], np.asarray(L1_gnn_upd_w2)]
    rows = [*np.asarray(L0_gnn_lin_b), *np.asarray(L0_gnn_linl_b), np.asarray(L1_gnn_msg_b1),
            np.asarray(L1_gnn_msg_b2), np.asarray(L1_gnn_upd_b2)]
    cols = [*np.asarray(L0_gnn_ln_g), *np.asarray(L0_gnn_ln_b), np.asarray(L1_gnn_upd_b1),
            np.asarray(L1_gnn_msg_b2)]
    arrays = {
        "x": padded(x, NPAD),
        "src": by_edge(srcs),
        "dst": by_edge(dsts),
        "dst_t": np.ascontiguousarray(dsts.transpose(0, 2, 1)).reshape(NG, GE),
        "dst_g": np.ascontiguousarray(dsts.reshape(NG, GE)),
        "edge_attr": padded(edge_attr_128, EPAD),
        "consts": consts,
        "mats": np.ascontiguousarray(np.stack(mats, axis=1)),
        "rows": np.stack(rows),
        "cols": np.ascontiguousarray(np.stack(cols, axis=1)),
    }
    nc = bacc.Bacc("TRN2", target_bir_lowering=False, num_devices=1)
    ins = [nc.dram_tensor(n, a.shape, mybir.dt.from_np(a.dtype), kind="ExternalInput").ap() for n, a in arrays.items()]
    out = nc.dram_tensor("out", (NPAD, D), F32, kind="ExternalOutput").ap()
    gnn_kernel(nc, *ins, out)
    r = run_bass_kernel_spmd(nc, [arrays], core_ids=[0])
    return r.results[0]["out"][:N]
```

```python
from contextlib import ExitStack

import numpy as np

import concourse.bass as bass
from concourse import mybir

N, D, E = 6250, 128, 106250
P = 128
NT = -(-N // P)
NPAD = NT * P
K = 8
GE = P * K
RING = 4
NG = RING * (-(-E // (GE * RING)))
EPAD = NG * GE
SUPER = NG // RING
TB = 7
NB = NT // TB
BW = TB * P
assert NB * TB == NT
EPS = 1e-5

F32, BF16, I32 = mybir.dt.float32, mybir.dt.bfloat16, mybir.dt.int32
ALU, ACT, AX = mybir.AluOpType, mybir.ActivationFunctionType, mybir.AxisListType

C_IOTA, C_BASE, C_NODE, C_ID, C_END = 0, P, P + NT, P + 2 * NT, 2 * P + 2 * NT

MATS = ["lin0", "lin1", "lin2", "wl0", "wl1", "wl2", "wr0", "wr1", "wr2",
        "m_src", "m_dst", "m_edge", "m_w2", "u_x", "u_agg", "u_w2"]
ROWS = ["lin_b0", "lin_b1", "lin_b2", "wl_b0", "wl_b1", "wl_b2", "m_b1", "m_b2", "u_b2"]
COLS = ["g0", "g1", "b0", "b1", "u_b1", "m_b2"]

TIMES = {0: NB, 1: NT, 2: NT, 3: NT, 4: NB}
STEPS = {
    "mean": (1, 2, 3, 4),
    "zeroed": (1, 2, 3),
    "proj": (1, 2, 3, 4),
    "sum": (1, 2, 3),
    "relu": (1, 2),
    "keep": (3,),
    "stats": (0, 1, 2, 3),
    "std": (0, 1, 2, 3),
    "rstd": (0, 1, 2, 3),
    "norm": (0, 1, 2, 3),
    "turn": (0, 1, 2, 3),
    "feat": (0, 1, 2, 3),
    "table": (0, 1, 2, 3),
    "tabout": (0, 1, 2, 3),
    "own": (0, 1, 2, 3),
    "ownout": (0, 1, 2, 3),
    "split": (3,),
    "upx": (3,),
    "upxout": (3,),
    "bias": (4,),
    "aggout": (4,),
    "uagg": (4,),
    "usum": (4,),
    "urelu": (4,),
    "out": (4,),
    "outsb": (4,),
}


def done(step, phase, i):
    return sum(TIMES[q] for q in STEPS[step] if q < phase) + i + 1


def gnn_kernel(nc, x, src, dst, dst_t, dst_g, edge_attr, consts, mats, rows, cols, out):
    ctx = ExitStack()
    with ctx:
        def sb(name, shape, dt=F32):
            return ctx.enter_context(nc.sbuf_tensor(name, shape, dt))

        def sem(name):
            return ctx.enter_context(nc.semaphore(name))

        tables = [nc.dram_tensor(f"table{i}", (NPAD, D), F32).ap() for i in range(2)]
        x1_dram = nc.dram_tensor("x1_dram", (NPAD, D), F32).ap()
        win_dram = nc.dram_tensor("win_dram", (NG, 2), I32).ap()

        con = sb("con", [P, C_END])
        mat = sb("mat", [P, len(MATS), D])
        row = sb("row", [P, len(ROWS), D])
        col = sb("col", [P, len(COLS)])
        row_parts = sb("row_parts", [P, len(ROWS), D], BF16)
        row_sum = sb("row_sum", [P, P], BF16)
        ones = sb("ones", [P, P], BF16)
        zeros = sb("zeros", [P, P])
        eps = sb("eps", [P, 1])
        dst_i = sb("dst_i", [P, NG * K], I32)
        dst_f = sb("dst_f", [P, NG * K])
        win_m = sb("win_m", [NG, 2], I32)
        win_s = sb("win_s", [NG, 2], I32)
        win = sb("win", [1, NG, 4], I32)
        least = sb("least", [1, 2, 2 * P])

        agg = sb("agg", [P, NPAD])
        cnt = sb("cnt", [P, NPAD])
        own = sb("own", [P, NPAD])
        q_parts = sb("q_parts", [P, 3, NPAD], BF16)
        x_all = q_parts[:, 0:2, :].rearrange("p a n -> p (a n)").bitcast(F32)

        idx = sb("idx", [P, RING, K], I32)
        rows_g = sb("rows_g", [P, RING, K, D])
        onehot = sb("onehot", [P, 2, K, P])
        buf = sb("buf", [P, 8 * GE])
        dst_g_sb = buf[0:NG, 7 * GE:8 * GE].bitcast(I32)
        ea = [buf[:, i * GE:(i + 1) * GE] for i in range(2)]
        eat = buf[:, 2 * GE:3 * GE]
        dtb = [buf[:, i * GE:(i + 1) * GE].bitcast(I32) for i in (3, 4)]
        msg = [buf[:, i * GE:(i + 1) * GE] for i in (5, 6)]
        onehot_t = buf[:, 7 * GE:8 * GE].bitcast(BF16).rearrange("p (s e) -> p s e", s=2)
        y_b, *stage_b = (buf[:, i * GE:i * GE + BW] for i in range(3))
        row_rest = buf[:, 3 * GE:3 * GE + len(ROWS) * D].rearrange("p (r f) -> p r f", f=D)
        st6_b = sb("st6_b", [P, NT, 6])
        mv_b = sb("mv_b", [P, NT, 2])
        std_b = sb("std_b", [P, NT])
        rstd_b = sb("rstd_b", [P, NT])
        small = sb("small", [P, 10, D])
        mean, z, zr, y, feat, stage, res, keep, rest, rest2 = (small[:, i, :] for i in range(10))
        urelu_b = small[:, 0:TB, :].rearrange("p t f -> p (t f)")
        st6 = sb("st6", [P, 6])
        mv = sb("mv", [P, 2])
        std = sb("std", [P, 1])
        rstd = sb("rstd", [P, 1])

        def pb(name):
            return ctx.enter_context(nc.psum_tensor(name, [P, GE], F32))

        ps_h, ps_t, ps_x, ps_b = pb("ps_h"), pb("ps_t"), pb("ps_x"), pb("ps_b")
        ps_m = [ps_x, ps_b]
        ps_u = {1: ps_x, 2: ps_b, 3: ps_x}
        ps_a = ps_h[:, :].rearrange("p (s c) -> p s c", s=2)
        ps_c = ps_t[:, :].rearrange("p (s c) -> p s c", s=2)
        tp_h, tp_t, tp_x, tp_b = ps_x[:, 0:D], ps_x[:, GE // 2:GE // 2 + D], ps_b[:, 0:D], ps_b[:, GE // 2:GE // 2 + D]

        in_con = sem("in_con")
        in_row = sem("in_row")
        in_mat = sem("in_mat")
        in_dst = sem("in_dst")
        in_dstg = sem("in_dstg")
        row_split = sem("row_split")
        rows_split = sem("rows_split")
        ready = sem("ready")
        win_made = sem("win_made")
        win_out = sem("win_out")
        win_in = sem("win_in")
        win_done = sem("win_done")
        st = {k: sem("n_" + k) for k in STEPS}
        chain = sem("chain")
        in_x = [sem(f"in_x{b}") for b in range(NB)]
        res_in = sem("res_in")
        tab_out = sem("tab_out")
        blk_out = [sem("blk_out0"), sem("blk_out1")]
        x1_out = sem("x1_out")
        final_out = sem("final_out")
        idx_in = [sem(f"idx_in{s}") for s in range(RING)]
        gathered = [sem(f"gathered{s}") for s in range(RING)]
        passed = sem("passed")
        rows_used = sem("rows_used")
        hot = sem("hot")
        summed = sem("summed")
        added = sem("added")
        cleared = sem("cleared")
        ea_in = [sem("ea_in0"), sem("ea_in1")]
        dt_in = [sem("dt_in0"), sem("dt_in1")]
        turned = sem("turned")
        eat_made = sem("eat_made")
        hot_t = sem("hot_t")
        q_added = sem("q_added")
        m_done = sem("m_done")
        m_sum = sem("m_sum")
        m_relu = sem("m_relu")
        msg_used = sem("msg_used")

        M = {k: mat[:, i, :] for i, k in enumerate(MATS)}
        R = {k: row_parts[:, i, :] for i, k in enumerate(ROWS)}
        RB = {k: row[:, i, :] for i, k in enumerate(ROWS)}
        C = {k: col[:, i:i + 1] for i, k in enumerate(COLS)}
        ident = con[:, C_ID:C_ID + P]

        def tile(t, i):
            return t[:, bass.ds(i * P, P)]

        def blk(t, b):
            return t[:, bass.ds(b * BW, BW)]

        def dram_blk(t, b):
            return t[bass.ds(b * BW, BW), :].rearrange("(t p) f -> p t f", p=P)

        def tiles(t):
            return t.rearrange("p (t f) -> p t f", f=P)

        class Windows:

            def __init__(self, eng, name):
                self.eng = eng
                self.now = [eng.alloc_register(f"{name}_win{i}") for i in range(4 * RING)]
                self.old = [eng.alloc_register(f"{name}_old{i}") for i in range(9)]
                self.tile = eng.alloc_register(f"{name}_tile")

            def start(self):
                for r in (*self.now[4 * (RING - 3):], self.tile):
                    self.eng.reg_mov(r, 0)

            def load(self, j):
                for i, r in enumerate(self.old):
                    self.eng.reg_mov(r, self.now[4 * (RING - 3 + i // 3) + i % 3])
                self.eng.load(self.now, win[0:1, bass.ds(j * RING, RING), :].rearrange("o g c -> o (g c)"))

            def regs(self, s):
                return self.now[4 * s:4 * s + 3] if s >= 0 else self.old[3 * (s + 3):3 * (s + 3) + 3]

            def of(self, s):
                lo, hi, _ = self.regs(s)
                return (self.eng.snap(lo, min_val=0, max_val=NT - 1), self.eng.snap(hi, min_val=1, max_val=NT))

            def at(self):
                return self.eng.snap(self.tile, min_val=0, max_val=NT - 1)

            def at_block(self):
                return self.eng.snap(self.tile, min_val=0, max_val=NB - 1)

            def ready(self, s):
                return self.eng.snap(self.tile, min_val=0, max_val=NT) < \
                    self.eng.snap(self.regs(s)[2], min_val=0, max_val=NT)

            def block_ready(self, s):
                return self.eng.snap(self.tile, min_val=0, max_val=NB) * TB + TB - 1 < \
                    self.eng.snap(self.regs(s)[2], min_val=0, max_val=NT)

            def next(self):
                self.eng.reg_add(self.tile, self.tile, 1)

        def blocks_stored(eng):
            for i in range(2):
                eng.wait_ge(blk_out[i], (NB - i + 1) // 2 * 16)

        SPLIT_STEPS = 6

        def split_rows(eng, which, split):
            parts, rest_of = row_parts[:, which, :], row_rest[:, which, :]
            second, third = slice(32, 64), slice(64, 96)
            eng.tensor_scalar(parts, row[:, which, :], 1.0, None, ALU.mult).then_inc(split, 1)
            eng.wait_ge(split, 1)
            eng.tensor_tensor(rest_of, row[:, which, :], parts, ALU.subtract).then_inc(split, 1)
            eng.wait_ge(split, 2)
            eng.tensor_scalar(parts[second], rest_of[second], 1.0, None, ALU.mult).then_inc(split, 1)
            eng.wait_ge(split, 3)
            eng.tensor_scalar(parts[third], rest_of[third], 1.0, None, ALU.mult).then_inc(split, 1)
            eng.wait_ge(split, 4)
            eng.tensor_tensor(rest_of[third], rest_of[third], parts[third], ALU.subtract).then_inc(split, 1)
            eng.wait_ge(split, 5)
            eng.tensor_scalar(parts[third], rest_of[third], 1.0, None, ALU.mult).then_inc(split, 1)
            eng.wait_ge(split, SPLIT_STEPS)

        block = ctx.enter_context(nc.Block())

        @block.sync
        def _(sp):
            def load_x(b):
                sp.dma_start(tiles(blk(x_all, b)), dram_blk(x, b)).then_inc(in_x[b], 16)

            load_x(0)
            sp.dma_start(con[:, :], consts).then_inc(in_con, 16)
            sp.dma_start(row[:, :, :], rows.partition_broadcast(P)).then_inc(in_row, 16)
            load_x(1)
            sp.dma_start(mat[:, :, :], mats).then_inc(in_mat, 16)
            sp.dma_start(col[:, :], cols).then_inc(in_mat, 16)
            for b in range(2, NB):
                load_x(b)
            sp.dma_start(dst_g_sb, dst_g).then_inc(in_dstg, 16)
            sp.dma_start(dst_i[:, :], dst).then_inc(in_dst, 16)
            for b in range(NB):
                sp.wait_ge(st["tabout"], b + 1)
                sp.dma_start(dram_blk(tables[0], b), tiles(stage_b[b % 2])).then_inc(blk_out[b % 2], 16)

            for l in range(4):
                if l == 3:
                    blocks_stored(sp)
                with sp.Fori(0, SUPER) as j:
                    for s in range(RING):
                        g = j * RING + s
                        sp.wait_ge(gathered[s], (l * SUPER + j) * 16 * K)
                        sp.sem_inc(passed, 1)
                        sp.dma_start(idx[:, s, :], src[:, bass.ds(g * K, K)]).then_inc(idx_in[s], 16)
                        if l == 3:
                            sp.wait_ge(turned, g + 1)
                            sp.sem_inc(passed, 1)
                            sp.dma_start(ea[s % 2].rearrange("p (k f) -> p k f", f=D),
                                         edge_attr[bass.ds(g * GE, GE), :].rearrange("(p k) f -> p k f", k=K)) \
                                .then_inc(ea_in[s % 2], 16)
                            sp.wait_ge(m_done, g + 1)
                            sp.sem_inc(passed, 1)
                            sp.dma_start(dtb[s % 2], dst_t[bass.ds(g, 1), :].partition_broadcast(P)) \
                                .then_inc(dt_in[s % 2], 16)
            sp.wait_ge(final_out, 16 * NB)

        @block.gpsimd
        def _(pool):
            pool.wait_ge(in_row, 16)
            split_rows(pool, slice(1, len(ROWS)), rows_split)
            pool.memset(cnt[:, :], 0.0)
            pool.memset(agg[:, :], 0.0).then_inc(cleared, 1)
            pool.sem_inc(rows_used, RING)
            pool.sem_inc(m_relu, RING)
            for l in range(4):
                if l == 0:
                    blocks_stored(pool)
                else:
                    pool.wait_ge(tab_out, 16 * l * NT)
                if l == 3:
                    pool.wait_ge(rows_used, 3 * NG + RING)
                with pool.Fori(0, SUPER) as j:
                    for s in range(RING):
                        if l < 3:
                            pool.wait_ge(rows_used, (l * SUPER + j) * RING + s + 1)
                        else:
                            pool.wait_ge(m_relu, j * RING + s + 1)
                        pool.wait_ge(idx_in[s], (l * SUPER + j + 1) * 16)
                        pool.sem_inc(passed, 1)
                        for k in range(K):
                            pool.indirect_dma_start(
                                rows_g[:, s, k, :], None, tables[l % 2],
                                bass.IndirectOffsetOnAxis(ap=idx[:, s, k:k + 1], axis=0),
                            ).then_inc(gathered[s], 16)

        @block.tensor
        def _(pe):
            w = Windows(pe, "pe")
            visit = pe.alloc_register("pe_visit")
            qvisit = pe.alloc_register("pe_qvisit")
            pe.reg_mov(visit, 0)
            pe.reg_mov(qvisit, 0)
            for s in (summed, turned, q_added, m_done, msg_used):
                pe.sem_inc(s, 2)
            pe.wait_ge(in_con, 16)
            pe.wait_ge(ready, 1)

            def signal(s, at, start=True):
                nc.tensor.matmul(at, zeros[0:1, 0:1], zeros[0:1, 0:1], start=start, stop=True,
                                 skip_group_check=not start).then_inc(s, 1)

            def zero_visit(l):
                v = pe.snap(visit, min_val=0, max_val=1 << 20)
                pe.wait_ge(added, v + 1)
                if l == 0:
                    nc.tensor.matmul(ps_c[:, bass.ds(v % 2, 1), 0:P], zeros[:, :], zeros[:, :], start=True, stop=True)
                nc.tensor.matmul(ps_a[:, bass.ds(v % 2, 1), 0:P], zeros[:, :], zeros[:, :],
                                 start=True, stop=True).then_inc(summed, 1)
                pe.reg_add(visit, visit, 1)

            def sum_visits(l, window, rows_of, rows_sem, rows_value):
                pe.wait_ge(rows_sem, rows_value)
                pe.sem_inc(passed, 1)
                with pe.Fori(*window):
                    v = pe.snap(visit, min_val=0, max_val=1 << 20)
                    pe.wait_ge(hot, v + 1)
                    pe.wait_ge(added, v + 1)
                    hs = onehot[:, bass.ds(v % 2, 1), :, :]
                    if l == 0:
                        halves = hs.bitcast(BF16).rearrange("p s k (n h) -> p s k n h", h=2)[:, :, :, :, 1]
                        for k in range(K):
                            nc.tensor.matmul(ps_c[:, bass.ds(v % 2, 1), 0:P], ones[:, :], halves[:, :, k, :],
                                             start=(k == 0), stop=(k == K - 1))
                    for k in range(K):
                        last = nc.tensor.matmul(ps_a[:, bass.ds(v % 2, 1), 0:P], rows_of(k), hs[:, :, k, :],
                                                start=(k == 0), stop=(k == K - 1))
                    last.then_inc(summed, 1)
                    pe.reg_add(visit, visit, 1)

            HALF = [(0, 512), (512, BW)]

            def block_products(dst_ps, lhs, rhs, s):
                for t in range(TB):
                    last = nc.tensor.matmul(dst_ps[:, t * P:(t + 1) * P], lhs[:, t * P:(t + 1) * P], M[rhs],
                                            start=True, stop=True)
                last.then_inc(st[s], 1)

            def turn_block(b):
                pe.wait_ge(st["norm"], b + 1)
                if b >= 1:
                    pe.wait_ge(st["feat"], b)
                for t in range(TB):
                    last = nc.tensor.transpose(ps_t[:, t * P:(t + 1) * P], y_b[:, t * P:(t + 1) * P], ident)
                last.then_inc(st["turn"], 1)

            def biased_products(acc, b, weight, bias, step):
                for t in range(TB):
                    at = acc[:, t * P:(t + 1) * P]
                    nc.tensor.matmul(at, tile(x_all, b * TB + t), M[weight], start=True, stop=False)
                    last = nc.tensor.matmul(at, row_sum[:, :], R[bias], start=False, stop=True)
                last.then_inc(st[step], 1)

            def project_block(b):
                pe.wait_ge(st["feat"], b + 1)
                pe.wait_ge(row_split, SPLIT_STEPS)
                pe.wait_ge(in_mat, 32)
                if b >= 2:
                    pe.wait_ge(st["tabout"], b - 1)
                biased_products(ps_m[b % 2], b, "lin0", "lin_b0", "table")

            turn_block(0)
            for b in range(NB):
                if b + 1 < NB:
                    turn_block(b + 1)
                project_block(b)
            pe.wait_ge(st["feat"], NB)
            zero_visit(0)
            pe.wait_ge(rows_split, SPLIT_STEPS)
            for b in range(NB):
                pe.wait_ge(st["tabout"], min(NB, NB - 1 + b))
                if b >= 2:
                    pe.wait_ge(st["ownout"], b - 1)
                biased_products(ps_m[(NB + b) % 2], b, "wr0", "wl_b0", "own")
            def node_front(ph, t):
                pe.wait_ge(st["mean"], done("mean", ph, t))
                pe.wait_ge(st["sum"], done("sum", ph, t) - 1)
                if ph == 1:
                    pe.wait_ge(st["ownout"], NB)
                if ph == 3:
                    pe.wait_ge(st["upxout"], t)
                nc.tensor.matmul(tp_h, mean[:, :], M[f"wl{ph - 1}"], start=True, stop=True).then_inc(st["proj"], 1)

            def node_back(ph, t):
                pe.wait_ge(st["norm"], done("norm", ph, t))
                pe.wait_ge(st["feat"], done("feat", ph, t) - 1)
                nc.tensor.transpose(tp_t, y[:, :], ident).then_inc(st["turn"], 1)
                pe.wait_ge(st["feat"], done("feat", ph, t))
                pe.wait_ge(st["tabout"], done("tabout", ph, t) - 1)
                if ph < 3:
                    nc.tensor.matmul(tp_x, feat[:, :], M[f"lin{ph}"], start=True, stop=False)
                    nc.tensor.matmul(tp_x, row_sum[:, :], R[f"lin_b{ph}"], start=False, stop=True) \
                        .then_inc(st["table"], 1)
                else:
                    nc.tensor.matmul(tp_x, feat[:, :], M["m_src"], start=True, stop=True).then_inc(st["table"], 1)
                pe.wait_ge(st["ownout"], done("ownout", ph, t) - 1)
                nc.tensor.matmul(tp_b, feat[:, :], M[f"wr{ph}" if ph < 3 else "m_dst"], start=True, stop=False)
                nc.tensor.matmul(tp_b, row_sum[:, :], R[f"wl_b{ph}" if ph < 3 else "m_b1"], start=False, stop=True) \
                    .then_inc(st["own"], 1)
                if ph == 3:
                    nc.tensor.matmul(tp_h, M["u_x"], feat[:, :], start=True, stop=True).then_inc(st["upx"], 1)

            pe.wait_ge(win_done, 1)
            def groups(l, j, spread):
                w.load(j)
                for s in range(RING):
                    with pe.If(w.ready(s - 2)):
                        node_front(l + 1, w.at())
                        if not spread:
                            node_back(l + 1, w.at())
                            w.next()
                    sum_visits(l, w.of(s), lambda k: rows_g[:, s, k, :], gathered[s], (l * SUPER + j + 1) * 16 * K)
                    pe.drain().then_inc(rows_used, 1)
                    if spread:
                        with pe.If(w.ready(s - 2)):
                            node_back(l + 1, w.at())
                            w.next()

            for l in range(3):
                w.start()
                with pe.Fori(0, SUPER) as j:
                    groups(l, j, l == 0)
                zero_visit(l + 1)
                with pe.Fori(w.at(), NT) as t:
                    node_front(l + 1, t)
                    node_back(l + 1, t)

            pe.wait_ge(st["split"], NT + 1)
            for k in ("feat", "tabout", "ownout", "upxout"):
                pe.wait_ge(st[k], done(k, 3, NT - 1))

            def edge_front(m, s):
                pe.wait_ge(ea_in[s % 2], (m - s) * 8 + (s // 2) * 16 + 16)
                pe.wait_ge(eat_made, m)
                for k in range(K):
                    last = nc.tensor.transpose(ps_t[:, k * P:(k + 1) * P], ea[s % 2][:, k * P:(k + 1) * P], ident)
                last.then_inc(turned, 1)

            def edge_products(m, s):
                acc = ps_m[s % 2]
                pe.wait_ge(m_sum, m + 1)
                pe.wait_ge(eat_made, m + 1)
                for k in range(K):
                    nc.tensor.matmul(acc[:, k * P:(k + 1) * P], eat[:, k * P:(k + 1) * P], M["m_edge"],
                                     start=(k % 4 == 0), stop=(k % 4 == 3), skip_group_check=True)

            def node_products(s):
                acc = ps_m[s % 2]
                with pe.Fori(*w.of(s)) as n:
                    q = pe.snap(qvisit, min_val=0, max_val=1 << 20)
                    pe.wait_ge(hot_t, q + 1)
                    for k in range(K):
                        for part in range(3):
                            last = nc.tensor.matmul(
                                acc[:, k * P:(k + 1) * P], onehot_t[:, bass.ds(q % 2, 1), k * P:(k + 1) * P],
                                q_parts[:, part, bass.ds(n * P, P)], start=False, stop=True, skip_group_check=True)
                    last.then_inc(q_added, 1)
                    pe.reg_add(qvisit, qvisit, 1)
                signal(m_done, acc[0:1, GE - 1:GE], start=False)

            def edge_sum(a, s):
                sum_visits(3, w.of(s - 2), lambda k: msg[s % 2][:, k * P:(k + 1) * P], m_relu, a + 1 + RING)
                signal(msg_used, ps_m[s % 2][0:1, 0:1])

            def update_product(b, step):
                if step == 3:
                    pe.wait_ge(st["urelu"], b + 1)
                    block_products(ps_u[step], urelu_b, "u_w2", "out")
                else:
                    if step == 1:
                        pe.wait_ge(st["mean"], done("mean", 4, b))
                    else:
                        pe.wait_ge(st["aggout"], b + 1)
                    for a, c in HALF:
                        last = nc.tensor.matmul(ps_u[step][:, a:c], M["m_w2" if step == 1 else "u_agg"],
                                                agg[:, bass.ds(b * BW + a, c - a)], start=True, stop=True)
                    last.then_inc(st["proj" if step == 1 else "uagg"], 1)

            def message_group(m, s, earlier=True, update=True):
                edge_front(m, s)
                if earlier:
                    edge_sum(m - 2, s)
                if update and s >= 1:
                    with pe.If(w.block_ready(-3)):
                        pe.wait_ge(m_sum, m + 2)
                        update_product(w.at_block(), s)
                        if s == 3:
                            w.next()
                if update and s == 0:
                    pe.wait_ge(st["outsb"], w.at_block())
                edge_products(m, s)
                node_products(s)

            w.start()
            w.load(0)
            for m in range(RING):
                message_group(m, m, m >= 2, False)
            with pe.Fori(1, SUPER) as j:
                w.load(j)
                for s in range(RING):
                    message_group(j * RING + s, s)
            for s in range(2):
                sum_visits(3, w.of(RING - 2 + s), lambda k: msg[s % 2][:, k * P:(k + 1) * P],
                           m_relu, NG - 2 + s + 1 + RING)
            pe.wait_ge(m_sum, NG + 2)
            with pe.Fori(w.at_block(), NB) as b:
                for step in (1, 2, 3):
                    update_product(b, step)

        @block.scalar
        def _(act):
            w = Windows(act, "act")
            act.wait_ge(ready, 1)

            def std_block(b):
                act.wait_ge(st["stats"], b + 1)
                at = slice(b * TB, (b + 1) * TB)
                nc.scalar.activation(std_b[:, at], mv_b[:, at, 1], ACT.Sqrt, bias=eps[:, 0:1]).then_inc(st["std"], 1)

            def feat_block(b):
                act.wait_ge(st["turn"], b + 1)
                nc.scalar.activation(blk(x_all, b), ps_t[:, 0:BW], ACT.Relu).then_inc(st["feat"], 1)

            def table_block(b):
                act.wait_ge(st["table"], b + 1)
                if b >= 2:
                    act.wait_ge(blk_out[b % 2], b // 2 * 16)
                nc.scalar.activation(stage_b[b % 2], ps_m[b % 2][:, 0:BW], ACT.Relu).then_inc(st["tabout"], 1)

            std_block(0)
            for b in range(NB):
                if b + 1 < NB:
                    std_block(b + 1)
                feat_block(b)
                if b >= 1:
                    table_block(b - 1)
            act.wait_ge(win_made, 1)
            act.dma_start(win_dram, win_s[:, :]).then_inc(win_out, 16)
            table_block(NB - 1)
            act.wait_ge(win_out, 16)
            act.dma_start(win[:, :, 0:2], win_dram.rearrange("(o g) c -> o g c", o=1)).then_inc(win_in, 16)
            for b in range(NB):
                act.wait_ge(st["own"], b + 1)
                nc.scalar.activation(blk(own, b), ps_m[(NB + b) % 2][:, 0:BW], ACT.Copy).then_inc(st["ownout"], 1)

            def node_tile(ph, t):
                def rows_of(dram):
                    return dram[bass.ds(t * P, P), :]

                if ph == 3:
                    act.wait_ge(st["sum"], done("sum", 3, t) - 1)
                    act.dma_start(res[:, :], rows_of(x)).then_inc(res_in, 16)
                act.wait_ge(st["stats"], done("stats", ph, t))
                nc.scalar.activation(std[:, :], mv[:, 1:2], ACT.Sqrt, bias=eps[:, 0:1]).then_inc(st["std"], 1)
                if ph == 3:
                    act.wait_ge(st["keep"], t + 1)
                    act.dma_start(rows_of(x1_dram), keep[:, :]).then_inc(x1_out, 16)
                act.wait_ge(st["turn"], done("turn", ph, t))
                act.wait_ge(st["own"], done("own", ph, t) - 1)
                if ph == 3:
                    act.wait_ge(st["upx"], t)
                    nc.scalar.activation(feat[:, :], tp_t, ACT.Relu).then_inc(st["feat"], 1)
                else:
                    nc.scalar.activation(feat[:, :], tp_t, ACT.Identity, bias=C[f"b{ph - 1}"],
                                         scale=C[f"g{ph - 1}"]).then_inc(st["feat"], 1)
                act.wait_ge(st["table"], done("table", ph, t))
                act.wait_ge(tab_out, ((ph - 1) * NT + t) * 16)
                nc.scalar.activation(stage[:, :], tp_x, ACT.Relu if ph < 3 else ACT.Copy).then_inc(st["tabout"], 1)
                act.wait_ge(st["tabout"], done("tabout", ph, t))
                act.dma_start(rows_of(tables[ph % 2]), stage[:, :]).then_inc(tab_out, 16)
                act.wait_ge(st["own"], done("own", ph, t))
                if ph < 3:
                    act.wait_ge(st["sum"], done("sum", ph, t))
                    act.sem_inc(passed, 1)
                    nc.scalar.activation(tile(own, t), tp_b, ACT.Copy).then_inc(st["ownout"], 1)
                else:
                    act.wait_ge(st["split"], t)
                    nc.scalar.activation(rest[:, :], tp_b, ACT.Copy).then_inc(st["ownout"], 1)
                    act.wait_ge(st["upx"], t + 1)
                    act.sem_inc(passed, 1)
                    nc.scalar.activation(tile(own, t), tp_h, ACT.Copy).then_inc(st["upxout"], 1)

            act.wait_ge(win_done, 1)
            act.wait_ge(in_mat, 32)
            for l in range(3):
                w.start()
                with act.Fori(0, SUPER) as j:
                    w.load(j)
                    for s in range(RING):
                        with act.If(w.ready(s - 2)):
                            node_tile(l + 1, w.at())
                            w.next()
                with act.Fori(w.at(), NT) as t:
                    node_tile(l + 1, t)

            def eat_group(m):
                act.wait_ge(turned, m + 3)
                act.wait_ge(m_done, m + 2)
                nc.scalar.activation(eat, ps_t[:, :], ACT.Copy).then_inc(eat_made, 1)

            def relu_group(m, s):
                act.wait_ge(m_sum, m + 3)
                act.wait_ge(msg_used, m + 1)
                nc.scalar.activation(msg[s % 2], rows_g[:, s, :, :].rearrange("p k f -> p (k f)"), ACT.Relu) \
                    .then_inc(m_relu, 1)

            def update_load(b):
                act.wait_ge(st["aggout"], b + 1)
                act.sem_inc(passed, 1)
                act.dma_start(tiles(blk(cnt, b)), dram_blk(x1_dram, b)).then_inc(res_in, 16)

            def update_relu(b):
                act.wait_ge(st["usum"], b + 1)
                nc.scalar.activation(urelu_b, blk(own, b), ACT.Relu, bias=C["u_b1"]).then_inc(st["urelu"], 1)

            def update_store(b):
                act.wait_ge(st["outsb"], b + 1)
                act.sem_inc(passed, 1)
                act.dma_start(dram_blk(out, b), tiles(blk(agg, b))).then_inc(final_out, 16)

            def message_group(m, s, after=True):
                if s == 2:
                    with act.If(w.block_ready(-3)):
                        update_load(w.at_block())
                if s == 3:
                    with act.If(w.block_ready(-3)):
                        update_relu(w.at_block())
                if after:
                    eat_group(m + 1)
                relu_group(m, s)
                if s == 3:
                    with act.If(w.block_ready(-3)):
                        update_store(w.at_block())
                        w.next()

            act.wait_ge(st["own"], done("own", 3, NT - 1))
            act.wait_ge(st["upx"], NT)
            act.wait_ge(st["sum"], done("sum", 3, NT - 1))
            act.wait_ge(x1_out, 16 * NT)
            w.start()
            w.load(0)
            eat_group(0)
            for m in range(RING):
                eat_group(m + 1)
                relu_group(m, m)
            with act.Fori(1, SUPER - 1) as j:
                w.load(j)
                for s in range(RING):
                    message_group(j * RING + s, s)
            w.load(SUPER - 1)
            for s in range(RING):
                message_group(NG - RING + s, s, s < RING - 1)
            with act.Fori(w.at_block(), NB) as b:
                update_load(b)
                update_relu(b)
                update_store(b)

        @block.vector
        def _(dve):
            w = Windows(dve, "dve")
            links = [0]

            def link(ins):
                links[0] += 1
                ins.then_inc(chain, 1)
                dve.wait_ge(chain, links[0])

            visit = dve.alloc_register("dve_visit")
            qvisit = dve.alloc_register("dve_qvisit")
            prev = dve.alloc_register("dve_prev")
            for r in (visit, qvisit, prev):
                dve.reg_mov(r, 0)
            dve.sem_inc(added, 2)
            dve.sem_inc(m_sum, 2)
            dve.memset(zeros[:, :], 0.0)
            dve.memset(ones[:, :], 1.0)
            link(dve.memset(row_sum[:, :], 0.0))
            for i in range(3):
                dve.memset(row_sum[32 * i:32 * i + 1, :], 1.0)
            dve.memset(rest[:, :], 0.0)
            dve.memset(win[:, :, :], 0)
            dve.memset(least[:, :, :], float(NT))
            dve.memset(eps[:, :], EPS).then_inc(ready, 1)

            def stats_block(b):
                dve.wait_ge(in_x[b], 16)
                for t in range(b * TB, (b + 1) * TB):
                    last = dve.bn_stats(st6_b[:, t, :], x_all[:, t * P:(t + 1) * P])
                link(last)
                for t in range(b * TB, (b + 1) * TB):
                    last = dve.bn_aggr(mv_b[:, t, :], st6_b[:, t, :])
                last.then_inc(st["stats"], 1)

            def norm_block(b):
                at = slice(b * TB, (b + 1) * TB)
                dve.wait_ge(st["std"], b + 1)
                dve.reciprocal(rstd_b[:, at], std_b[:, at]).then_inc(st["rstd"], 1)
                dve.wait_ge(st["rstd"], b + 1)
                dve.wait_ge(st["stats"], b + 1)
                if b >= 1:
                    dve.wait_ge(st["turn"], b)
                for t in range(TB):
                    at = b * TB + t
                    last = dve.tensor_scalar(y_b[:, t * P:(t + 1) * P], tile(x_all, at),
                                             mv_b[:, at:at + 1, 0], rstd_b[:, at:at + 1], ALU.subtract, ALU.mult)
                last.then_inc(st["norm"], 1)

            stats_block(0)
            for b in range(NB):
                if b + 1 < NB:
                    stats_block(b + 1)
                norm_block(b)
                if b == 0:
                    dve.wait_ge(in_row, 16)
                    split_rows(dve, slice(0, 1), row_split)
            dve.wait_ge(in_dstg, 16)
            dve.tensor_reduce(win_m[:, 0:1], dst_g_sb, AX.X, ALU.min)
            link(dve.tensor_reduce(win_m[:, 1:2], dst_g_sb, AX.X, ALU.max))
            link(dve.tensor_scalar(win_s[:, :], win_m[:, :], 7, None, ALU.arith_shift_right))
            dve.tensor_scalar(win_s[:, 1:2], win_s[:, 1:2], 1.0, None, ALU.add).then_inc(win_made, 1)
            dve.wait_ge(in_dst, 16)
            link(dve.tensor_copy(dst_f[:, :], dst_i[:, :]))
            dve.wait_ge(win_in, 16)
            link(dve.tensor_copy(least[:, 0, 0:NG - 1], win[:, 1:NG, 0]))
            step, at = 1, 0
            while step < NG:
                link(dve.tensor_tensor(least[:, 1 - at, 0:P], least[:, at, 0:P], least[:, at, step:step + P], ALU.min))
                step, at = 2 * step, 1 - at
            dve.tensor_copy(win[:, :, 2], least[:, at, 0:NG]).then_inc(win_done, 1)
            dve.wait_ge(win_done, 1)
            dve.wait_ge(cleared, 1)
            dve.wait_ge(in_con, 16)
            dve.wait_ge(in_mat, 32)

            def add_last(l, v):
                dve.wait_ge(summed, v + 2)
                dve.wait_ge(added, v + 1)
                at = dve.snap(prev, min_val=0, max_val=NPAD - P)
                if l == 0:
                    c = cnt[:, bass.ds(at, P)].rearrange("p (a n) -> p a n", a=1)
                    dve.tensor_tensor(c, c, ps_c[:, bass.ds((v + 1) % 2, 1), 0:P], ALU.add)
                a = agg[:, bass.ds(at, P)].rearrange("p (a n) -> p a n", a=1)
                dve.tensor_tensor(a, a, ps_a[:, bass.ds((v + 1) % 2, 1), 0:P], ALU.add).then_inc(added, 1)

            def hot_visits(l, window, g):
                with dve.Fori(*window) as n:
                    v = dve.snap(visit, min_val=1, max_val=1 << 20)
                    dve.wait_ge(summed, v + 1)
                    dve.scalar_tensor_tensor(
                        onehot[:, bass.ds(v % 2, 1), :, :].rearrange("p s k n -> p (s k) n"),
                        con[:, C_IOTA:C_IOTA + P].rearrange("p (a n) -> p a n", a=1).broadcast_to([P, K, P]),
                        con[:, bass.ds(n + C_BASE, 1)],
                        dst_f[:, bass.ds(g * K, K)].rearrange("p (k a) -> p k a", a=1).broadcast_to([P, K, P]),
                        ALU.add, ALU.is_equal).then_inc(hot, 1)
                    add_last(l, v)
                    dve.reg_mov(prev, n * P)
                    dve.reg_add(visit, visit, 1)

            def zero_visit():
                dve.sem_inc(hot, 1)
                dve.reg_mov(prev, 0)
                dve.reg_add(visit, visit, 1)

            PER = {1: 3, 2: 1, 3: 5}
            within = {ph: sem(f"within{ph}") for ph in PER}

            def links_of(ph, t, before):
                step = [before]

                def then(ins):
                    step[0] += 1
                    ins.then_inc(within[ph], 1)
                    dve.wait_ge(within[ph], t * PER[ph] + step[0])
                return then

            def split(t, then):
                part = [q_parts[:, i, bass.ds(t, P)] for i in range(3)]
                then(dve.tensor_scalar(part[0], rest[:, :], 1.0, None, ALU.mult))
                then(dve.tensor_tensor(rest2[:, :], rest[:, :], part[0], ALU.subtract))
                then(dve.tensor_scalar(part[1], rest2[:, :], 1.0, None, ALU.mult))
                dve.tensor_tensor(part[2], rest2[:, :], part[1], ALU.subtract).then_inc(st["split"], 1)

            last_tile = dve.alloc_register("dve_last_tile")
            dve.reg_mov(last_tile, 0)

            def node_front(ph, t):
                then = links_of(ph, t, 0)
                c = tile(cnt, t)
                if ph == 1:
                    then(dve.tensor_scalar(c, c, 0.5, None, ALU.max))
                    dve.sem_inc(passed, 1)
                    then(dve.reciprocal(c, c))
                dve.wait_ge(st["proj"], done("proj", ph, t) - 1)
                dve.tensor_tensor(mean[:, :], tile(agg, t), c, ALU.mult).then_inc(st["mean"], 1)
                dve.wait_ge(st["mean"], done("mean", ph, t))
                dve.tensor_scalar(tile(agg, t), zeros[:, :], 0.0, None, ALU.add).then_inc(st["zeroed"], 1)
                if ph == 3:
                    dve.wait_ge(st["ownout"], done("ownout", 3, t) - 1)
                    at = dve.snap(last_tile, min_val=0, max_val=NPAD - P)
                    split(at, then)
                    dve.reg_mov(last_tile, t * P)

            def node_back(ph, t):
                then = links_of(ph, t, {1: 2, 2: 0, 3: 3}[ph])
                dve.wait_ge(st["ownout"], NB + (ph - 1) * NT)
                dve.wait_ge(st["proj"], done("proj", ph, t))
                if ph == 3:
                    dve.wait_ge(res_in, 16 * (t + 1))
                    then(dve.tensor_tensor(z[:, :], tp_h, tile(own, t), ALU.add))
                    dve.tensor_tensor(z[:, :], z[:, :], res[:, :], ALU.add).then_inc(st["sum"], 1)
                    dve.wait_ge(st["sum"], done("sum", ph, t))
                else:
                    dve.tensor_tensor(z[:, :], tp_h, tile(own, t), ALU.add).then_inc(st["sum"], 1)
                    dve.wait_ge(st["sum"], done("sum", ph, t))
                    dve.tensor_scalar(zr[:, :], z[:, :], 0.0, None, ALU.max).then_inc(st["relu"], 1)
                    dve.wait_ge(st["relu"], done("relu", ph, t))
                zz = z if ph == 3 else zr
                then(dve.bn_stats(st6[:, :], zz[:, :]))
                dve.sem_inc(passed, 1)
                dve.bn_aggr(mv[:, :], st6[:, :]).then_inc(st["stats"], 1)
                dve.wait_ge(st["stats"], done("stats", ph, t))
                if ph == 3:
                    dve.wait_ge(x1_out, 16 * t)
                    dve.tensor_tensor(keep[:, :], z[:, :], RB["u_b2"], ALU.add).then_inc(st["keep"], 1)
                dve.wait_ge(st["std"], done("std", ph, t))
                dve.reciprocal(rstd[:, :], std[:, :]).then_inc(st["rstd"], 1)
                dve.wait_ge(st["rstd"], done("rstd", ph, t))
                dve.wait_ge(st["turn"], done("turn", ph, t) - 1)
                dve.tensor_scalar(y[:, :], zz[:, :], mv[:, 0:1], rstd[:, 0:1], ALU.subtract, ALU.mult) \
                    .then_inc(st["norm"], 1)

            def groups(l, j, spread):
                w.load(j)
                for s in range(RING):
                    with dve.If(w.ready(s - 2)):
                        node_front(l + 1, w.at())
                        if not spread:
                            node_back(l + 1, w.at())
                            w.next()
                    hot_visits(l, w.of(s), j * RING + s)
                    if spread:
                        with dve.If(w.ready(s - 2)):
                            node_back(l + 1, w.at())
                            w.next()

            zero_visit()
            for l in range(3):
                w.start()
                with dve.Fori(0, SUPER) as j:
                    groups(l, j, l == 0)
                v = dve.snap(visit, min_val=1, max_val=1 << 20)
                add_last(l, v)
                dve.wait_ge(added, v + 2)
                zero_visit()
                with dve.Fori(w.at(), NT) as t:
                    node_front(l + 1, t)
                    node_back(l + 1, t)
                dve.wait_ge(st["zeroed"], (l + 1) * NT)

            dve.wait_ge(st["ownout"], done("ownout", 3, NT - 1))
            dve.wait_ge(st["split"], NT)
            split((NT - 1) * P, link)

            def hot_t_visits(m, s):
                dve.wait_ge(dt_in[s % 2], (m - s) * 8 + (s // 2) * 16 + 16)
                dve.sem_inc(passed, 1)
                with dve.Fori(*w.of(s)) as n:
                    q = dve.snap(qvisit, min_val=0, max_val=1 << 20)
                    dve.wait_ge(q_added, q + 1)
                    dve.tensor_scalar(onehot_t[:, bass.ds(q % 2, 1), :],
                                      dtb[s % 2].rearrange("p (a e) -> p a e", a=1),
                                      con[:, bass.ds(n + C_NODE, 1)], None, ALU.is_equal).then_inc(hot_t, 1)
                    dve.reg_add(qvisit, qvisit, 1)

            def add_rows(m, s):
                dve.wait_ge(m_done, m + 3)
                dve.wait_ge(gathered[s], (m - s) * 32 + (3 * SUPER + 1) * 16 * K)
                r = rows_g[:, s, :, :].rearrange("p k f -> p (k f)")
                dve.tensor_tensor(r, ps_m[s % 2][:, :], r, ALU.add).then_inc(m_sum, 1)

            def update_step(b, step):
                if step == 0:
                    dve.tensor_tensor(blk(agg, b), blk(agg, b), blk(cnt, b), ALU.mult).then_inc(st["mean"], 1)
                    dve.wait_ge(st["mean"], done("mean", 4, b))
                    dve.tensor_scalar(blk(cnt, b), blk(cnt, b), 1.5, C["m_b2"], ALU.is_lt, ALU.mult) \
                        .then_inc(st["bias"], 1)
                elif step == 1:
                    dve.wait_ge(st["proj"], done("proj", 4, b))
                    dve.wait_ge(st["bias"], b + 1)
                    dve.tensor_tensor(blk(agg, b), ps_u[step][:, 0:BW], blk(cnt, b), ALU.add) \
                        .then_inc(st["aggout"], 1)
                elif step == 2:
                    dve.wait_ge(st["uagg"], b + 1)
                    dve.tensor_tensor(blk(own, b), ps_u[step][:, 0:BW], blk(own, b), ALU.add).then_inc(st["usum"], 1)
                else:
                    dve.wait_ge(st["out"], b + 1)
                    dve.wait_ge(res_in, 16 * (NT + 1 + b))
                    dve.tensor_tensor(blk(agg, b), ps_u[step][:, 0:BW], blk(cnt, b), ALU.add) \
                        .then_inc(st["outsb"], 1)

            def message_group(m, s, earlier=True, update=True):
                hot_t_visits(m, s)
                if update:
                    with dve.If(w.block_ready(-3)):
                        update_step(w.at_block(), s)
                        if s == 3:
                            w.next()
                if earlier:
                    hot_visits(3, w.of(s - 1), m - 1)
                add_rows(m, s)

            dve.wait_ge(st["upxout"], NT)
            dve.wait_ge(tab_out, 16 * 3 * NT)
            w.start()
            w.load(0)
            for m in range(RING):
                message_group(m, m, m >= 1, False)
            with dve.Fori(1, SUPER) as j:
                w.load(j)
                for s in range(RING):
                    message_group(j * RING + s, s)
            hot_visits(3, w.of(RING - 1), NG - 1)
            v = dve.snap(visit, min_val=1, max_val=1 << 20)
            add_last(3, v)
            dve.wait_ge(added, v + 2)
            dve.sem_inc(passed, 1)
            with dve.Fori(w.at_block(), NB) as b:
                for step in range(4):
                    update_step(b, step)


def kernel(x, src, dst, edge_attr_128, L0_gnn_lin_w, L0_gnn_lin_b, L0_gnn_linl_w, L0_gnn_linl_b, L0_gnn_linr_w,
           L0_gnn_ln_g, L0_gnn_ln_b, L1_gnn_msg_w1, L1_gnn_msg_b1, L1_gnn_msg_w2, L1_gnn_msg_b2,
           L1_gnn_upd_w1, L1_gnn_upd_b1, L1_gnn_upd_w2, L1_gnn_upd_b2):
    import concourse.bacc as bacc
    from concourse.bass_utils import run_bass_kernel_spmd

    def padded(a, n, fill=0):
        a = np.asarray(a)
        p = np.full((n,) + a.shape[1:], fill, a.dtype)
        p[:a.shape[0]] = a
        return p

    srcs = padded(src, EPAD).astype(np.int32).reshape(NG, P, K)
    dsts = padded(dst, EPAD, NPAD - 1).astype(np.int32).reshape(NG, P, K)
    by_edge = lambda a: np.ascontiguousarray(a.transpose(1, 0, 2)).reshape(P, NG * K)
    consts = np.zeros((P, C_END), np.float32)
    consts[:, C_IOTA:C_IOTA + P] = np.arange(P)
    consts[:, C_BASE:C_BASE + NT] = np.arange(NT) * P
    consts[:, C_NODE:C_NODE + NT] = np.arange(NT) * P + np.arange(P)[:, None]
    consts[:, C_ID:C_ID + P] = np.eye(P)
    lin, wl, wr = (np.asarray(a).transpose(0, 2, 1) for a in (L0_gnn_lin_w, L0_gnn_linl_w, L0_gnn_linr_w))
    w1, u1 = np.asarray(L1_gnn_msg_w1), np.asarray(L1_gnn_upd_w1)
    mats = [*lin, *wl, *wr, w1[:D], w1[D:2 * D], w1[2 * D:], np.asarray(L1_gnn_msg_w2),
            u1[:D], u1[D:], np.asarray(L1_gnn_upd_w2)]
    rows = [*np.asarray(L0_gnn_lin_b), *np.asarray(L0_gnn_linl_b), np.asarray(L1_gnn_msg_b1),
            np.asarray(L1_gnn_msg_b2), np.asarray(L1_gnn_upd_b2)]
    cols = [*np.asarray(L0_gnn_ln_g), *np.asarray(L0_gnn_ln_b), np.asarray(L1_gnn_upd_b1),
            np.asarray(L1_gnn_msg_b2)]
    arrays = {
        "x": padded(x, NPAD),
        "src": by_edge(srcs),
        "dst": by_edge(dsts),
        "dst_t": np.ascontiguousarray(dsts.transpose(0, 2, 1)).reshape(NG, GE),
        "dst_g": np.ascontiguousarray(dsts.reshape(NG, GE)),
        "edge_attr": padded(edge_attr_128, EPAD),
        "consts": consts,
        "mats": np.ascontiguousarray(np.stack(mats, axis=1)),
        "rows": np.stack(rows),
        "cols": np.ascontiguousarray(np.stack(cols, axis=1)),
    }
    nc = bacc.Bacc("TRN2", target_bir_lowering=False, num_devices=1)
    ins = [nc.dram_tensor(n, a.shape, mybir.dt.from_np(a.dtype), kind="ExternalInput").ap() for n, a in arrays.items()]
    out = nc.dram_tensor("out", (NPAD, D), F32, kind="ExternalOutput").ap()
    gnn_kernel(nc, *ins, out)
    r = run_bass_kernel_spmd(nc, [arrays], core_ids=[0])
    return r.results[0]["out"][:N]
```
